# Optimizing a Trainium2 kernel written in Bass

```python
import numpy as np
import jax
import jax.numpy as jnp

def _softmax(x, axis=-1):
    return jax.nn.softmax(x, axis=axis)

def _gelu(x):
    return jax.nn.gelu(x, approximate=True)

def _silu(x):
    return jax.nn.silu(x)

def _sigmoid(x):
    return jax.nn.sigmoid(x)

def _layernorm(x, axis=-1, eps=1e-05):
    m = jnp.mean(x, axis=axis, keepdims=True)
    v = jnp.var(x, axis=axis, keepdims=True)
    return (x - m) / jnp.sqrt(v + eps)

def _scatter_add(tgt, idx, src, axis=0):
    return tgt.at[idx].add(src)

def _segment_sum(src, seg, n):
    return jax.ops.segment_sum(src, seg, n)
kernel_name = 'mk_cond_seq_d2_seqx_r4_610567'

def setup_inputs(seed: int=0):
    np.random.seed(seed)
    _w = jnp.asarray

    def _rec_inputs():
        import jax
        import jax.numpy as jnp
        _rk = jax.random.key(seed)
        x = -9.26e-05 + 0.9999 * jax.random.normal(jax.random.fold_in(_rk, 1), (8, 256, 288), jnp.float32)
        _lenS = 256 - jax.random.randint(jax.random.fold_in(_rk, 7), (8,), 0, max(1, 256 // 4) + 1, jnp.int32)
        _lenS2 = 256 - jax.random.randint(jax.random.fold_in(_rk, 8), (8,), 0, max(1, 256 // 4) + 1, jnp.int32)
        cond_1152 = 0.00338249 + 1.00093 * jax.random.normal(jax.random.fold_in(_rk, 11), (8, 288), jnp.float32)
        return (x, cond_1152)
    x, cond_1152 = _rec_inputs()

    def _L0_cond_setup():
        import jax, jax.numpy as jnp
        import numpy as np
        N, T, D, H = (32, 256, 288, 16)
        DH = D // H
        MLP = int(D * 4.0)
        EPS = 1e-06

        def _layernorm(x):
            m = jnp.mean(x, axis=-1, keepdims=True)
            v = jnp.var(x, axis=-1, keepdims=True)
            return (x - m) * jax.lax.rsqrt(v + EPS)

        def _modulate(x, shift, scale):
            return x * (1.0 + scale[:, None, :]) + shift[:, None, :]

        def _attention(x, qkv_w, qkv_b, proj_w, proj_b):
            n, t, d = x.shape
            scale = DH ** (-0.5)
            qkv = x @ qkv_w + qkv_b
            qkv = qkv.reshape(n, t, 3, H, DH)
            q, k, v = (qkv[:, :, 0], qkv[:, :, 1], qkv[:, :, 2])
            attn = jnp.einsum('nthd,ntkd->nthk', q * scale, k)
            attn = jax.nn.softmax(attn, axis=-1)
            out = jnp.einsum('nthk,ntkd->nthd', attn, v)
            out = out.transpose(0, 2, 1, 3).reshape(n, t, d)
            return out @ proj_w + proj_b

        def _mlp(x, fc1_w, fc1_b, fc2_w, fc2_b):
            h = jax.nn.gelu(x @ fc1_w + fc1_b, approximate=False)
            return h @ fc2_w + fc2_b
        key = jax.random.key(seed)
        ks = jax.random.split(key, 14)
        s = 0.02
        return {'x': jax.random.normal(ks[0], (N, T, D), jnp.float32), 'c': jax.random.normal(ks[1], (N, D), jnp.float32), 'qkv_w': jax.random.normal(ks[2], (D, 3 * D), jnp.float32) * s, 'qkv_b': jax.random.normal(ks[3], (3 * D,), jnp.float32) * s, 'proj_w': jax.random.normal(ks[4], (D, D), jnp.float32) * s, 'proj_b': jax.random.normal(ks[5], (D,), jnp.float32) * s, 'fc1_w': jax.random.normal(ks[6], (D, MLP), jnp.float32) * s, 'fc1_b': jax.random.normal(ks[7], (MLP,), jnp.float32) * s, 'fc2_w': jax.random.normal(ks[8], (MLP, D), jnp.float32) * s, 'fc2_b': jax.random.normal(ks[9], (D,), jnp.float32) * s, 'ada_w': jax.random.normal(ks[10], (D, 6 * D), jnp.float32) * s, 'ada_b': jax.random.normal(ks[11], (6 * D,), jnp.float32) * s}
    _L0_cond_all = _L0_cond_setup()
    _L0_cond_in = {k: v for k, v in _L0_cond_all.items() if k in ('qkv_w', 'qkv_b', 'proj_w', 'proj_b', 'fc1_w', 'fc1_b', 'fc2_w', 'fc2_b', 'ada_w', 'ada_b')}
    del _L0_cond_all

    def _L1_cond_setup():
        import jax, jax.numpy as jnp
        import numpy as np
        DIM = 288
        HEADS = 16
        HEAD_DIM = DIM // HEADS
        HIDDEN = int(DIM * 4.0)
        EPS = 1e-12

        def rmsnorm(x, g, d):
            n = jnp.linalg.norm(x, axis=-1, keepdims=True)
            return x / jnp.maximum(n, EPS) * d ** 0.5 * g

        def modulate(x, scale, shift):
            return x * (1.0 + scale[:, None, :]) + shift[:, None, :]
        key = jax.random.key(seed)
        ks = jax.random.split(key, 12)
        B, N = (8, 256)
        s = 0.02
        return {'x': jax.random.normal(ks[0], (B, N, DIM), jnp.float32), 'c': jax.random.normal(ks[1], (B, DIM), jnp.float32), 'g1': jnp.ones((1,), jnp.float32), 'g2': jnp.ones((1,), jnp.float32), 'qkv_w': jax.random.normal(ks[2], (3 * DIM, DIM), jnp.float32) * s, 'qkv_b': jnp.zeros((3 * DIM,), jnp.float32), 'qg': jnp.ones((1,), jnp.float32), 'kg': jnp.ones((1,), jnp.float32), 'proj_w': jax.random.normal(ks[3], (DIM, DIM), jnp.float32) * s, 'proj_b': jnp.zeros((DIM,), jnp.float32), 'fc1_w': jax.random.normal(ks[4], (HIDDEN, DIM), jnp.float32) * s, 'fc1_b': jnp.zeros((HIDDEN,), jnp.float32), 'fc2_w': jax.random.normal(ks[5], (DIM, HIDDEN), jnp.float32) * s, 'fc2_b': jnp.zeros((DIM,), jnp.float32), 'ada_w': jax.random.normal(ks[6], (6 * DIM, DIM), jnp.float32) * s, 'ada_b': jnp.zeros((6 * DIM,), jnp.float32)}
    _L1_cond_all = _L1_cond_setup()
    _L1_cond_in = {k: v for k, v in _L1_cond_all.items() if k in ('g1', 'g2', 'qkv_w', 'qkv_b', 'qg', 'kg', 'proj_w', 'proj_b', 'fc1_w', 'fc1_b', 'fc2_w', 'fc2_b', 'ada_w', 'ada_b')}
    del _L1_cond_all
    return {'x': x, 'cond_1152': cond_1152, 'L0_cond_qkv_w': _L0_cond_in['qkv_w'], 'L0_cond_qkv_b': _L0_cond_in['qkv_b'], 'L0_cond_proj_w': _L0_cond_in['proj_w'], 'L0_cond_proj_b': _L0_cond_in['proj_b'], 'L0_cond_fc1_w': _L0_cond_in['fc1_w'], 'L0_cond_fc1_b': _L0_cond_in['fc1_b'], 'L0_cond_fc2_w': _L0_cond_in['fc2_w'], 'L0_cond_fc2_b': _L0_cond_in['fc2_b'], 'L0_cond_ada_w': _L0_cond_in['ada_w'], 'L0_cond_ada_b': _L0_cond_in['ada_b'], 'L1_cond_g1': _L1_cond_in['g1'], 'L1_cond_g2': _L1_cond_in['g2'], 'L1_cond_qkv_w': _L1_cond_in['qkv_w'], 'L1_cond_qkv_b': _L1_cond_in['qkv_b'], 'L1_cond_qg': _L1_cond_in['qg'], 'L1_cond_kg': _L1_cond_in['kg'], 'L1_cond_proj_w': _L1_cond_in['proj_w'], 'L1_cond_proj_b': _L1_cond_in['proj_b'], 'L1_cond_fc1_w': _L1_cond_in['fc1_w'], 'L1_cond_fc1_b': _L1_cond_in['fc1_b'], 'L1_cond_fc2_w': _L1_cond_in['fc2_w'], 'L1_cond_fc2_b': _L1_cond_in['fc2_b'], 'L1_cond_ada_w': _L1_cond_in['ada_w'], 'L1_cond_ada_b': _L1_cond_in['ada_b']}

def reference(x, cond_1152, L0_cond_qkv_w, L0_cond_qkv_b, L0_cond_proj_w, L0_cond_proj_b, L0_cond_fc1_w, L0_cond_fc1_b, L0_cond_fc2_w, L0_cond_fc2_b, L0_cond_ada_w, L0_cond_ada_b, L1_cond_g1, L1_cond_g2, L1_cond_qkv_w, L1_cond_qkv_b, L1_cond_qg, L1_cond_kg, L1_cond_proj_w, L1_cond_proj_b, L1_cond_fc1_w, L1_cond_fc1_b, L1_cond_fc2_w, L1_cond_fc2_b, L1_cond_ada_w, L1_cond_ada_b):
    import jax
    import jax.numpy as jnp

    def _L0_cond_ref(x, c, qkv_w, qkv_b, proj_w, proj_b, fc1_w, fc1_b, fc2_w, fc2_b, ada_w, ada_b):
        import jax, jax.numpy as jnp
        import numpy as np
        N, T, D, H = (32, 256, 288, 16)
        DH = D // H
        MLP = int(D * 4.0)
        EPS = 1e-06

        def _layernorm(x):
            m = jnp.mean(x, axis=-1, keepdims=True)
            v = jnp.var(x, axis=-1, keepdims=True)
            return (x - m) * jax.lax.rsqrt(v + EPS)

        def _modulate(x, shift, scale):
            return x * (1.0 + scale[:, None, :]) + shift[:, None, :]

        def _attention(x, qkv_w, qkv_b, proj_w, proj_b):
            n, t, d = x.shape
            scale = DH ** (-0.5)
            qkv = x @ qkv_w + qkv_b
            qkv = qkv.reshape(n, t, 3, H, DH)
            q, k, v = (qkv[:, :, 0], qkv[:, :, 1], qkv[:, :, 2])
            attn = jnp.einsum('nthd,ntkd->nthk', q * scale, k)
            attn = jax.nn.softmax(attn, axis=-1)
            out = jnp.einsum('nthk,ntkd->nthd', attn, v)
            out = out.transpose(0, 2, 1, 3).reshape(n, t, d)
            return out @ proj_w + proj_b

        def _mlp(x, fc1_w, fc1_b, fc2_w, fc2_b):
            h = jax.nn.gelu(x @ fc1_w + fc1_b, approximate=False)
            return h @ fc2_w + fc2_b
        ada = jax.nn.silu(c) @ ada_w + ada_b
        shift_msa, scale_msa, gate_msa, shift_mlp, scale_mlp, gate_mlp = jnp.split(ada, 6, axis=1)
        x = x + gate_msa[:, None, :] * _attention(_modulate(_layernorm(x), shift_msa, scale_msa), qkv_w, qkv_b, proj_w, proj_b)
        x = x + gate_mlp[:, None, :] * _mlp(_modulate(_layernorm(x), shift_mlp, scale_mlp), fc1_w, fc1_b, fc2_w, fc2_b)
        return x

    def _L1_cond_ref(x, c, g1, g2, qkv_w, qkv_b, qg, kg, proj_w, proj_b, fc1_w, fc1_b, fc2_w, fc2_b, ada_w, ada_b):
        import jax, jax.numpy as jnp
        import numpy as np
        DIM = 288
        HEADS = 16
        HEAD_DIM = DIM // HEADS
        HIDDEN = int(DIM * 4.0)
        EPS = 1e-12

        def rmsnorm(x, g, d):
            n = jnp.linalg.norm(x, axis=-1, keepdims=True)
            return x / jnp.maximum(n, EPS) * d ** 0.5 * g

        def modulate(x, scale, shift):
            return x * (1.0 + scale[:, None, :]) + shift[:, None, :]
        B, N, D = x.shape
        mod = jax.nn.silu(c) @ ada_w.T + ada_b
        shift_msa, scale_msa, gate_msa, shift_mlp, scale_mlp, gate_mlp = jnp.split(mod, 6, axis=-1)
        gate_msa = jnp.tanh(gate_msa)
        gate_mlp = jnp.tanh(gate_mlp)
        h = modulate(rmsnorm(x, g1, D), scale_msa, shift_msa)
        qkv = h @ qkv_w.T + qkv_b
        qkv = qkv.reshape(B, N, 3, HEADS, HEAD_DIM).transpose(2, 0, 3, 1, 4)
        q, k, v = (qkv[0], qkv[1], qkv[2])
        q = rmsnorm(q, qg, HEAD_DIM)
        k = rmsnorm(k, kg, HEAD_DIM)
        q = q * HEAD_DIM ** (-0.5)
        attn = jax.nn.softmax(jnp.einsum('bhqd,bhkd->bhqk', q, k), axis=-1)
        o = jnp.einsum('bhqk,bhkd->bhqd', attn, v)
        o = o.transpose(0, 2, 1, 3).reshape(B, N, D)
        o = o @ proj_w.T + proj_b
        x = x + gate_msa[:, None, :] * o
        h2 = modulate(rmsnorm(x, g2, D), scale_mlp, shift_mlp)
        m = jax.nn.gelu(h2 @ fc1_w.T + fc1_b, approximate=True) @ fc2_w.T + fc2_b
        x = x + gate_mlp[:, None, :] * m
        return x
    x = _L0_cond_ref(x, cond_1152, L0_cond_qkv_w, L0_cond_qkv_b, L0_cond_proj_w, L0_cond_proj_b, L0_cond_fc1_w, L0_cond_fc1_b, L0_cond_fc2_w, L0_cond_fc2_b, L0_cond_ada_w, L0_cond_ada_b)
    x = _L1_cond_ref(x, cond_1152, L1_cond_g1, L1_cond_g2, L1_cond_qkv_w, L1_cond_qkv_b, L1_cond_qg, L1_cond_kg, L1_cond_proj_w, L1_cond_proj_b, L1_cond_fc1_w, L1_cond_fc1_b, L1_cond_fc2_w, L1_cond_fc2_b, L1_cond_ada_w, L1_cond_ada_b)
    return x

_drawn_inputs = setup_inputs


def setup_inputs(seed=0):
    import zlib

    import numpy as np

    out = dict(_drawn_inputs(seed))
    spreads = {'L1_cond_qkv_b': (0.0, 0.8),
     'L1_cond_proj_b': (0.0, 0.375),
     'L1_cond_fc1_b': (0.0, 0.8),
     'L1_cond_fc2_b': (0.0, 0.396),
     'L1_cond_ada_b': (0.0, 0.442)}
    factors = {'L0_cond_qkv_w': 8.0,
     'L0_cond_qkv_b': 8.0,
     'L0_cond_proj_w': 8.0,
     'L0_cond_proj_b': 8.0,
     'L0_cond_fc1_b': 50.967,
     'L0_cond_fc2_b': 8.0,
     'L0_cond_ada_b': 8.0,
     'L1_cond_qkv_w': 8.0,
     'L1_cond_proj_w': 6.16,
     'L0_cond_fc1_w': 3.962,
     'L0_cond_fc2_w': 3.107}
    for name, (base, spread) in spreads.items():
        noise = np.random.default_rng([zlib.crc32(name.encode()), seed]).standard_normal(out[name].shape)
        drawn = base * np.exp(spread * noise) if base else spread * noise
        out[name] = jnp.asarray(drawn.astype(out[name].dtype))
    for name, factor in factors.items():
        out[name] = (out[name] * factor).astype(out[name].dtype)
    return out
```

```python
from contextlib import ExitStack

import numpy as np
import concourse.bass as bass
from concourse import mybir

F32 = mybir.dt.float32
F32R = mybir.dt.float32r
U32 = mybir.dt.uint32
I32 = mybir.dt.int32
ALU = mybir.AluOpType
ACT = mybir.ActivationFunctionType
AX = mybir.AxisListType

P = 128
NB = 8
FREE = 2
TOK = 256
NT = TOK // P
D = 288
H = 16
DH = D // H
F = 4 * D
NM = F // P
REM = D - 2 * P
KREM = 3 * REM + 2
BH = 7
BLK = BH * DH
TAILH = H - 2 * BH
TAIL = BLK - TAILH * DH
KSUM = 96
GH = 4
NG = H // GH
SLOTS = 16
TG = TOK // 32
NGT = TOK // TG
MROW = 3 * DH
BIG = 2.0 ** 100
ADA_KIND = 2 * P + 3 * REM
ADA = 4 * ADA_KIND + 2 * D
EPS0 = 1e-6
EPS1 = 1e-12
LN_SET = "natural_log_exp_and_others"

BANK_MAX, BANK_ST, BANK_AV, BANK_A, BANK_C = (0, 1), (2, 3), 4, (5, 6), 7
BANK_F1, BANK_F2 = (0, 1, 2), (3, 4)


def wait(eng, sem, value):
    if isinstance(value, int) and value <= 0:
        return
    eng.wait_ge(sem, value)


def held(eng, value):
    return value if isinstance(value, int) else eng.to_reg(value)


class Batch:

    def __init__(self, layer, pair, offset):
        self.pair, self.par = pair + offset // 2, offset % 2
        self.first = isinstance(self.pair, int) and self.pair == 0 and self.par == 0
        b = self.pair * 2 + self.par
        self.n = b + layer * NB
        self.qa = b + 2 * layer * NB
        self.qm = b + (2 * layer + 1) * NB
        self.layer = layer
        self.b = b


def attention_steps(eng, step):
    for i in (-2, -1, 0):
        step(0, i)
    with eng.Fori(0, 2) as k:
        for i in (1, 2):
            step(k, i)
    for i in (5, 6, 7, 8):
        step(0, i)


def mlp_steps(eng, step):
    for i in (-2, -1, 0, 1):
        step(0, i)
    with eng.Fori(0, 2) as k:
        for i in (2, 3):
            step(k, i)
    for i in (6, 7):
        step(0, i)


def max_heads(s):
    return [h for h in range(H) if 3 + h * 13 // H == s]


def token_group(u, half, c):
    return 16 * half + GH * u + c


def build(nc, A, out):
    with ExitStack() as ctx:
        sb = lambda name, shape, dt=F32: ctx.enter_context(nc.sbuf_tensor(name, shape, dt))
        sem = lambda name: ctx.enter_context(nc.semaphore(name))

        x_sb = sb("x_sb", [P, NB // 2, 2, NT, D])
        ident = sb("ident", [P, P])
        sumsel = sb("sumsel", [P, P])
        mask_x = sb("mask_x", [P, 1])
        mask_w = sb("mask_w", [P, 1])
        gains = sb("gains", [P, 4])
        qk_gain = sb("qk_gain", [P, 2, 2])
        apart = sb("apart", [TG, 2, TOK])
        apart_r = sb("apart_r", [TG, 2, TOK], F32R)
        neg_half = sb("neg_half", [P, NT])
        floor = sb("floor", [P, 2, NT])
        mod = sb("mod", [P, 2, 4, 3, NB // 2, 2])
        s_c = sb("s_c", [P, 3, NB])
        wqkv = sb("wqkv", [P, 5, 3 * D], F32R)
        wproj = sb("wproj", [P, 2, NG, D], F32R)
        waits = sb("waits", [P, 1])
        bn = sb("bn", [P, NT, 6])
        mv = sb("mv", [P, NT, 2])
        vtmp = sb("vtmp", [P, NT])
        vtmp2 = sb("vtmp2", [P, NT])
        rstd = sb("rstd", [P, NT])
        z = sb("z", [P, NT, 2 * P + 3 * REM])
        y = sb("y", [P, 3, TOK])
        hs = sb("hs", [P, 2, 5, TOK], F32R)
        gate = sb("gate", [P, 2, D])
        res = sb("res", [P, NT, D])
        big = sb("big", [P, 2, 2, H * TOK], F32R)
        stack = big[:, :, :, :].rearrange("p a b (h t) -> p a b h t", h=H)
        flat = big[:, :, :, :].rearrange("p a b c -> p (a b c)")
        w1 = flat[:, 0:5 * F].rearrange("p (k n) -> p k n", k=5)
        w2 = flat[:, 5 * F:5 * F + 2 * NM * D].rearrange("p (s m n) -> p s m n", s=2, m=NM)

        with ExitStack() as at:
            sa = lambda name, shape, dt=F32: at.enter_context(nc.sbuf_tensor(name, shape, dt))
            prob = sa("prob", [P, 2 * GH, NT, TOK])
            qk_row = sa("qk_row", [P, NT, 2 * D])
            sq = sa("sq", [P, 2 * D])
            ss = sa("ss", [P, NT, 2 * H])
            rs = sa("rs", [P, NT, 2 * H])
            rt = sa("rt", [P, NT, 2 * H])
            qk_y = sa("qk_y", [P, 3, 2, TOK])
            qk_hi = sa("qk_hi", [P, 3, 2, TOK], F32R)
            qk_lo = sa("qk_lo", [P, 3, 2, TOK], F32R)
            v_sb = sa("v_sb", [P, 2, NT, H, 32])
            mx = sa("mx", [P, NT, H])
            negmax = sa("negmax", [8, 2, TOK], F32R)
            mx_tok = sa("mx_tok", [P, NGT])
            negmax_tok = sa("negmax_tok", [P, NGT], F32R)
            o_sb = sa("o_sb", [P, 2, TOK])
            lnsum = sa("lnsum", [P, TOK])
            recip = sa("recip", [P, 2, TOK])
            o_y = sa("o_y", [P, 2, TOK])
            o_hi = sa("o_hi", [P, NG, TOK], F32R)
            o_lo = sa("o_lo", [P, NG, TOK], F32R)
        with ExitStack() as ml:
            sm = lambda name, shape, dt=F32: ml.enter_context(nc.sbuf_tensor(name, shape, dt))
            stage = sm("stage", [P, 2, F])
            b2 = sm("b2", [P, D])
            g_y = sm("g_y", [P, 2, 3, TOK])
            g_hi = sm("g_hi", [P, 2, NM, TOK], F32R)
            g_lo = sm("g_lo", [P, 2, NM, TOK], F32R)
        with ExitStack() as ad:
            sd = lambda name, shape, dt=F32: ad.enter_context(nc.sbuf_tensor(name, shape, dt))
            stage_again = sd("stage_again", [P, 2, F])
            ada_w = sd("ada_w", [P, 3, ADA])
            ada_row = sd("ada_row", [NB, ADA])
            ada_b = sd("ada_b", [NB, 2, ADA])
            c_e = sd("c_e", [P, 3, NB])
            c_t = sd("c_t", [P, 3, NB])

        by_group = lambda rows, par, side, g: big[0:rows, par, side, g::NGT]
        v_rows = sq[:, :].rearrange("p (t d) -> p t d", t=NT)
        v_group = v_sb[:, :, :, :, :].rearrange("p a t h e -> p a (t h) e")
        v_dram = nc.dram_tensor("v_scratch", (2, TOK, D), F32, kind="Internal").ap()
        ps = ctx.enter_context(nc.psum_tensor("ps", [P, 8, 512], F32))
        gates_dram = nc.dram_tensor("gates_scratch", (2, NB, 2, D), F32, kind="Internal").ap()

        x_first, x_rest, const_in, ada_in = sem("x_first"), sem("x_rest"), sem("const_in"), sem("ada_in")
        ada_w_in, gain_set = sem("ada_w_in"), sem("gain_set")
        const_set, c_chain, v_ones = sem("const_set"), sem("c_chain"), sem("v_ones")
        ada_ps, ada_rowed, ada_tr, mod_set = sem("ada_ps"), sem("ada_rowed"), sem("ada_tr"), sem("mod_set")
        tanh_done, gates_out = sem("tanh_done"), sem("gates_out")
        w_in = [sem("w_in0"), sem("w_in1")]
        w_hi, w_lo = sem("w_hi"), sem("w_lo")
        b2_in = sem("b2_in")
        zeroed = sem("zeroed")
        bn_done, stats_done, var_done, rstd_done = sem("bn_done"), sem("stats_done"), sem("var_done"), sem("rstd_done")
        z_done, zt_ps, y_done = sem("z_done"), sem("zt_ps"), sem("y_done")
        hs_hi, hs_rem, hs_lo = sem("hs_hi"), sem("hs_rem"), sem("hs_lo")
        qk_ps, row_done, v_ps, v_done = sem("qk_ps"), sem("row_done"), sem("v_ps"), sem("v_done")
        vrow_out, v_in, mask_in = sem("vrow_out"), [sem("v_in0"), sem("v_in1")], sem("mask_in")
        apart_rounded = sem("apart_rounded")
        sq_done, ss_done, rs_chain, norm_done = sem("sq_done"), sem("ss_done"), sem("rs_chain"), sem("norm_done")
        qkt_ps, qky_done, qkhi_done, qklo_done = sem("qkt_ps"), sem("qky_done"), sem("qkhi_done"), sem("qklo_done")
        stack_in = [sem("stack_in0"), sem("stack_in1")]
        max_ps, max_done, maxt_ps, negmax_done = sem("max_ps"), sem("max_done"), sem("maxt_ps"), sem("negmax_done")
        maxrow_in = [sem("maxrow_in0"), sem("maxrow_in1")]
        st_ps, exp_done, av_ps, o_done = sem("st_ps"), sem("exp_done"), sem("av_ps"), sem("o_done")
        sum_ps, ln_done, recip_done = sem("sum_ps"), sem("ln_done"), sem("recip_done")
        oy_done, ohi_done, olo_done = sem("oy_done"), sem("ohi_done"), sem("olo_done")
        proj_ps, res_done, x_att = sem("proj_ps"), sem("res_done"), sem("x_att")
        gate_in = [sem("gate_in0"), sem("gate_in1")]
        f1_ps, gelu_done, ghi_done, glo_done = sem("f1_ps"), sem("gelu_done"), sem("ghi_done"), sem("glo_done")
        f2_ps, f2b_done, f2g_done, x_mlp = sem("f2_ps"), sem("f2b_done"), sem("f2g_done"), sem("x_mlp")
        out_done = sem("out_done")

        def chunks(layer, phase):
            if phase == 0:
                w = A[f"wqkv{layer}"]
                return [(w[:, 0, :], wqkv[:, 0, :], wqkv[:, 3, :]), (w[:, 1, :], wqkv[:, 1, :], wqkv[:, 4, :]),
                        (w[:, 2, :], wqkv[:, 2, :], None),
                        (A[f"wproj{layer}"].rearrange("p g n -> p (g n)"),
                         wproj[:, 0, :, :].rearrange("p g n -> p (g n)"),
                         wproj[:, 1, :, :].rearrange("p g n -> p (g n)"))]
            w = A[f"w1{layer}"]
            got = [(w[:, 0, :], w1[:, 0, :], w1[:, 3, :]), (w[:, 1, :], w1[:, 1, :], w1[:, 4, :]),
                   (w[:, 2, :], w1[:, 2, :], None)]
            for c in range(3):
                got.append((A[f"w2{layer}"][:, 3 * c:3 * c + 3, :].rearrange("p g n -> p (g n)"),
                            w2[:, 0, 3 * c:3 * c + 3, :].rearrange("p g n -> p (g n)"),
                            w2[:, 1, 3 * c:3 * c + 3, :].rearrange("p g n -> p (g n)")))
            return got

        def chunk_base(layer, phase):
            return 10 * layer + 4 * phase

        def chunk_end(layer, phase):
            return chunk_base(layer, phase) + (4 if phase == 0 else 6)

        def stack_count(B, back):
            use = B.pair + 4 * B.layer + (1 if B.par or not back else 0)
            return use * (18 * 16)

        def gate_count(B, phase):
            return (B.pair + (4 * (2 * B.layer + phase) + 1)) * 16

        def q_of(B, phase):
            return B.qa if phase == 0 else B.qm

        block = ctx.enter_context(nc.Block())

        @block.sync
        def _(sp):
            x_view = A["x"].rearrange("(k a) (t p) d -> p k a t d", a=2, p=P)
            out_view = out.rearrange("(k a) (t p) d -> p k a t d", a=2, p=P)
            gates_view = gates_dram.rearrange("l (k a) g d -> l k a g d", a=2)

            def load_weights(layer, phase):
                for c, (src, hi, _lo) in enumerate(chunks(layer, phase)):
                    k = chunk_base(layer, phase) + c
                    wait(sp, w_lo, k - 1)
                    sp.dma_start(stage[:, k % 2, 0:src.shape[1]], src).then_inc(w_in[k % 2], 16)

            def load_gate(B, phase):
                if phase == 0:
                    if isinstance(B.b, int) and B.b < 2:
                        wait(sp, f2g_done, NT * (NB * B.layer - 1 + B.b) if B.layer else 0)
                    else:
                        wait(sp, res_done, (B.n - 1) * NT)
                elif isinstance(B.b, int) and B.b < 2:
                    sp.wait_ge(res_done, NT * (NB * (B.layer + 1) - 1 + B.b))
                else:
                    wait(sp, f2g_done, (B.n - 1) * NT)
                sp.dma_start(gate[:, B.par, :],
                             gates_view[B.layer, B.pair, B.par, phase, :].partition_broadcast(P)
                             ).then_inc(gate_in[B.par], 16)

            def stack_block(B, blk, free):
                heads = slice(BH * blk, BH * blk + (BH if blk < 2 else TAILH))
                if blk < 2:
                    parts = [(0, 0, blk, 0), (1, 1, blk, 0)]
                else:
                    parts = [(0, 2, 0, TAIL), (1, 2, 1, TAIL)]
                for side, unit, half, first in parts:
                    made = held(sp, B.n * 3 + (unit + 1))
                    if side == 0:
                        wait(sp, st_ps, free)
                    sp.wait_ge(qkhi_done, made)
                    hi = qk_hi[first:BLK, unit, half, :].bitcast(F32)
                    lo = qk_lo[first:BLK, unit, half, :].bitcast(F32)
                    order = (hi, hi, lo) if side == 0 else (hi, lo, hi)
                    for r, part in enumerate(order):
                        if part is lo:
                            sp.wait_ge(qklo_done, made)
                        sp.dma_start(stack[DH * r:DH * r + DH, B.par, side, heads, :].bitcast(F32), part
                                     ).then_inc(stack_in[B.par], 16)

            def max_row(B, half):
                sp.wait_ge(negmax_done, B.n * 2 + (half + 1))
                sp.dma_start(stack[KSUM:KSUM + 1, B.par, 0, 8 * half:8 * half + 8, :].bitcast(F32),
                             negmax[:, half, :].bitcast(F32)).then_inc(maxrow_in[half], 16)

            def v_scatter(B):
                sp.wait_ge(v_done, (B.n + 1) * NT)
                sp.dma_start(v_dram[B.par].rearrange("(t p) d -> p t d", t=NT), v_rows[:, :, :]
                             ).then_inc(vrow_out, 16)
                sp.wait_ge(vrow_out, (B.n + 1) * 16)
                sp.dma_start(v_group[:, B.par, :, 0:DH],
                             v_dram[B.par].rearrange("(j g) (h d) -> h j g d", j=TG, h=H)).then_inc(v_in[B.par], 16)

            def max_row_tok(B):
                sp.wait_ge(negmax_done, B.n * 2 + 2)
                for half in range(2):
                    sp.dma_start(stack[KSUM:KSUM + 1, B.par, 0, 8 * half:8 * half + 8, :].bitcast(F32),
                                 negmax_tok[64 * half:64 * half + 64, :].bitcast(F32)).then_inc(maxrow_in[half], 16)

            def attention(layer):
                def step(k, i):
                    a, b, c = Batch(layer, k, i + 2), Batch(layer, k, i + 1), Batch(layer, k, i)
                    has_a, has_b, has_c = i + 2 <= 7, 0 <= i + 1 <= 7, 0 <= i <= 7
                    if has_c:
                        load_gate(c, 0)
                    if layer == 0:
                        if has_b:
                            v_scatter(b)
                        if has_a:
                            if i == -2:
                                sp.wait_ge(zeroed, 6)
                            for blk in range(3):
                                stack_block(a, blk, c.n * H + H if has_c else 0)
                        if has_b:
                            max_row_tok(b)
                        return
                    if has_a:
                        if i == -2:
                            sp.wait_ge(zeroed, 6 if layer == 0 else 10)
                        stack_block(a, 0, c.n * H + BH if has_c else 0)
                    if has_b:
                        max_row(b, 0)
                    if has_a:
                        stack_block(a, 1, c.n * H + 2 * BH if has_c else 0)
                    if has_b:
                        max_row(b, 1)
                    if has_a:
                        stack_block(a, 2, c.n * H + H if has_c else 0)
                attention_steps(sp, step)

            def mlp(layer):
                def step(k, i):
                    if i >= 0:
                        f = Batch(layer, k, i)
                        load_gate(f, 1)
                mlp_steps(sp, step)

            sp.dma_start(c_t[:, :, :], A["c_t"]).then_inc(ada_in, 16)
            sp.dma_start(ada_w[:, :, :], A["ada_w0"]).then_inc(ada_w_in, 16)
            sp.dma_start(x_sb[:, 0, :, :, :], x_view[:, 0, :, :, :]).then_inc(x_first, 16)
            sp.dma_start(ada_b[:, :, :], A["ada_b"]).then_inc(const_in, 16)
            sp.dma_start(ident[:, :], A["ident"]).then_inc(const_in, 16)
            sp.dma_start(sumsel[:, :], A["sumsel"]).then_inc(const_in, 16)
            sp.dma_start(mask_x[:, :], A["mask_x"]).then_inc(const_in, 16)
            sp.dma_start(mask_w[:, :], A["mask_w"]).then_inc(const_in, 16)
            sp.dma_start(gains[:, :], A["gains"]).then_inc(const_in, 16)
            sp.dma_start(apart[:, :, :], A["apart"]).then_inc(const_in, 16)
            load_weights(0, 0)
            sp.wait_ge(zeroed, 4)
            sp.wait_ge(apart_rounded, 1)
            for par in range(2):
                for side in range(2):
                    sp.dma_start(stack[MROW:MROW + TG, par, side, :, :].bitcast(F32),
                                 apart_r[:, side, :].bitcast(F32).unsqueeze(1).to_broadcast([TG, H, TOK])
                                 ).then_inc(mask_in, 16)
            for k in range(1, NB // 2):
                sp.dma_start(x_sb[:, k, :, :, :], x_view[:, k, :, :, :]).then_inc(x_rest, 16)
            sp.wait_ge(ada_rowed, 4)
            sp.dma_start(ada_w[:, :, :], A["ada_w1"]).then_inc(ada_w_in, 16)
            for layer in range(2):
                sp.wait_ge(ada_rowed, 4 * layer + 4)
                if layer == 1:
                    sp.wait_ge(tanh_done, 1)
                sp.dma_start(gates_dram[layer].rearrange("b g d -> b (g d)"),
                             ada_row[:, 4 * ADA_KIND:ADA]).then_inc(gates_out, 16)
                sp.wait_ge(gates_out, 16 * (layer + 1))
            for layer in range(2):
                attention(layer)
                sp.wait_ge(av_ps, NG * NB * (layer + 1))
                load_weights(layer, 1)
                sp.wait_ge(x_att, NT * NB * (layer + 1) + FREE)
                sp.dma_start(b2[:, :], A[f"b2{layer}"]).then_inc(b2_in, 16)
                mlp(layer)
                if layer == 0:
                    load_weights(1, 0)
            for k in range(NB // 2):
                sp.wait_ge(x_mlp, NT * (NB + 2 * k + 2))
                sp.dma_start(out_view[:, k, :, :, :], x_sb[:, k, :, :, :]).then_inc(out_done, 16)
            sp.wait_ge(out_done, 16 * (NB // 2))

        @block.gpsimd
        def _(pool):
            def norm_scale(B, phase):
                q = q_of(B, phase)
                pool.wait_ge(stats_done, (q + 1) * NT)
                wait(pool, z_done, q * NT * 2)
                if B.layer == 0:
                    pool.tensor_tensor(vtmp[:, :], mv[:, :, 1], floor[:, 0, :], ALU.add).then_inc(var_done, 1)
                    wait(pool, var_done, q + 1)
                else:
                    base = 2 * NB
                    pool.tensor_tensor(vtmp2[:, :], mv[:, :, 0], mv[:, :, 0], ALU.mult).then_inc(var_done, 1)
                    wait(pool, var_done, (q - base) * 3 + (base + 1))
                    pool.tensor_tensor(vtmp2[:, :], vtmp2[:, :], mv[:, :, 1], ALU.add).then_inc(var_done, 1)
                    wait(pool, var_done, (q - base) * 3 + (base + 2))
                    pool.tensor_tensor(floor[:, 1, :], neg_half[:, :], neg_half[:, :], ALU.mult)
                    pool.tensor_scalar(vtmp[:, :], vtmp2[:, :], EPS1 * EPS1 / D, None, ALU.max).then_inc(var_done, 1)
                    wait(pool, var_done, (q - base) * 3 + (base + 3))
                pool.tensor_tensor(rstd[:, :], vtmp[:, :], neg_half[:, :], ALU.pow).then_inc(rstd_done, 1)

            def h_lo(B, phase):
                q = q_of(B, phase)
                pool.wait_ge(hs_hi, q + 1)
                pool.tensor_tensor(hs[:, B.par, 3:5, :], y[:, 0:2, :], hs[:, B.par, 0:2, :].bitcast(F32),
                                   ALU.subtract).then_inc(hs_lo, 1)

            def qk_norm(B, t):
                m = B.n - NB
                pool.wait_ge(rs_chain, (m + 1) * 12)
                for side in range(2):
                    row = qk_row[:, t, side * D:side * D + 2 * BLK].rearrange("p (b d h) -> p b d h", b=2, d=DH)
                    r = rs[:, t, side * H:side * H + 2 * BH].rearrange("p (b h) -> p b h", b=2)
                    for b in range(2):
                        pool.tensor_tensor(row[:, b, :, :], row[:, b, :, :],
                                           r[:, b, :].unsqueeze(1).to_broadcast([P, DH, BH]), ALU.mult)
                    row = qk_row[:, t, side * D + 2 * BLK:(side + 1) * D].rearrange("p (d h) -> p d h", d=DH)
                    r = rs[:, t, side * H + 2 * BH:(side + 1) * H]
                    last = pool.tensor_tensor(row, row, r.unsqueeze(1).to_broadcast([P, DH, TAILH]), ALU.mult)
                last.then_inc(norm_done, 1)

            def qk_low(B, unit):
                rows = BLK
                pool.wait_ge(qkhi_done, B.n * 3 + (unit + 1))
                pool.tensor_tensor(qk_lo[0:rows, unit, :, :], qk_y[0:rows, unit, :, :],
                                   qk_hi[0:rows, unit, :, :].bitcast(F32), ALU.subtract).then_inc(qklo_done, 1)

            def o_low(B, g):
                pool.wait_ge(ohi_done, B.n * NG + (g + 1))
                pool.tensor_tensor(o_lo[:, g, :], o_y[:, g % 2, :], o_hi[:, g, :].bitcast(F32),
                                   ALU.subtract).then_inc(olo_done, 1)

            def add_attention(B, t):
                pool.wait_ge(res_done, B.n * NT + (t + 1))
                xt = x_sb[:, B.pair, B.par, t, :]
                pool.tensor_tensor(xt, xt, res[:, t, :], ALU.add).then_inc(x_att, 1)

            def attention(layer):
                def step(k, i):
                    a, c, t_ = Batch(layer, k, i + 2), Batch(layer, k, i), Batch(layer, k, i - 1)
                    has_a, has_c, has_t = i + 2 <= 7, 0 <= i <= 7, i >= 1
                    for s in range(SLOTS):
                        if has_a and s == 0:
                            norm_scale(a, 0)
                        if has_t and s == 2:
                            o_low(t_, 3)
                        if has_a and s == 4:
                            h_lo(a, 0)
                        if has_t and s in (5, 6):
                            add_attention(t_, s - 5)
                        if has_c and s in (7, 11, 15):
                            o_low(c, (s - 7) // 4)
                        if has_a and layer == 0 and s in (10, 11, 12):
                            qk_low(a, s - 10)
                        if has_a and layer == 1:
                            if s in (9, 10):
                                qk_norm(a, s - 9)
                            if s in (12, 13, 14):
                                qk_low(a, s - 12)
                attention_steps(pool, step)

            def g_low(B, j):
                pool.wait_ge(ghi_done, B.n * 3 + (j + 1))
                par = (B.par + j) % 2
                pool.tensor_tensor(g_lo[:, B.par, 3 * j:3 * j + 3, :], g_y[:, par, :, :],
                                   g_hi[:, B.par, 3 * j:3 * j + 3, :].bitcast(F32), ALU.subtract).then_inc(glo_done, 1)

            def add_mlp(B, t):
                pool.wait_ge(f2g_done, B.n * NT + (t + 1))
                xt = x_sb[:, B.pair, B.par, t, :]
                pool.tensor_tensor(xt, xt, res[:, t, :], ALU.add).then_inc(x_mlp, 1)

            def mlp(layer):
                def step(k, i):
                    d, e, f = Batch(layer, k, i + 2), Batch(layer, k, i + 1), Batch(layer, k, i)
                    if i + 2 <= 7:
                        norm_scale(d, 1)
                        h_lo(d, 1)
                    if 0 <= i + 1 <= 7:
                        g_low(e, 0)
                    if 0 <= i:
                        add_mlp(f, 0)
                    if 0 <= i + 1 <= 7:
                        g_low(e, 1)
                        g_low(e, 2)
                    if 0 <= i:
                        add_mlp(f, 1)
                mlp_steps(pool, step)

            pool.sem_inc(x_att, FREE)
            pool.memset(floor[:, 0, :], EPS0).then_inc(const_set, 1)
            pool.memset(neg_half[:, :], -0.5).then_inc(const_set, 1)
            pool.wait_ge(const_set, 2)
            for layer in range(2):
                if layer == 1:
                    pool.wait_ge(f2_ps, NT * NB)
                for par in range(2):
                    if layer == 0:
                        pool.memset(big[:, par, 0, :].bitcast(F32), 0.0).then_inc(zeroed, 1)
                    pool.memset(big[:, par, 1, :].bitcast(F32), 0.0).then_inc(zeroed, 1)
                pool.wait_ge(zeroed, 4 if layer == 0 else 8)
                for par in range(2):
                    pool.memset(big[KSUM:KSUM + 1, par, 1, :].bitcast(F32), 1.0).then_inc(zeroed, 1)
                    pool.wait_ge(zeroed, (4 if layer == 0 else 8) + par + 1)
                attention(layer)
                mlp(layer)

        @block.scalar
        def _(act):
            def split_hi(layer, phase):
                if phase == 1:
                    act.wait_ge(av_ps, NG * NB * (layer + 1))
                for c, (src, hi, _lo) in enumerate(chunks(layer, phase)):
                    k = chunk_base(layer, phase) + c
                    act.wait_ge(w_in[k % 2], 16 * (k // 2 + 1))
                    act.activation(hi, stage[:, k % 2, 0:src.shape[1]], ACT.Copy).then_inc(w_hi, 1)

            def modulate(B, phase):
                q = q_of(B, phase)
                wait(act, hs_rem, q)
                wait(act, hs_lo, q)
                for blk in range(3):
                    rows = P if blk < 2 else 3 * REM
                    act.wait_ge(zt_ps, q * 2 + (1 if blk < 2 else 2))
                    src = ps[0:rows, BANK_A[0], blk * TOK:(blk + 1) * TOK] if blk < 2 else ps[0:rows, BANK_A[1], 0:TOK]
                    act.activation(y[0:rows, blk, :], src, ACT.Identity,
                                   bias=mod[0:rows, B.layer, 2 * phase, blk, B.pair, B.par:B.par + 1],
                                   scale=mod[0:rows, B.layer, 2 * phase + 1, blk, B.pair, B.par:B.par + 1]
                                   ).then_inc(y_done, 1)

            def qk_out(B, t, side):
                act.wait_ge(qk_ps, B.n * 4 + (2 * t + side + 1))
                if t == 0 and side == 0:
                    wait(act, qkt_ps, B.n * 3)
                bank = BANK_A[side]
                act.activation(qk_row[:, t, side * D:(side + 1) * D], ps[:, bank, 0:D], ACT.Copy
                               ).then_inc(row_done, 1)

            def squares(B, t):
                m = B.n - NB
                act.wait_ge(row_done, B.n * 4 + (2 * t + 2))
                wait(act, ss_done, m * NT + t)
                act.activation(sq[:, :], qk_row[:, t, :], ACT.Square).then_inc(sq_done, 1)

            def heads_out(B, unit):
                act.wait_ge(qkt_ps, B.n * 3 + (unit + 1))
                wait(act, qklo_done, B.n * 3 - 2 + unit if isinstance(B.n, int) else B.n * 3 + (unit - 2))
                rows, bank = BLK, BANK_A[unit % 2]
                if unit < 2:
                    act.activation(qk_y[0:rows, unit, :, :].rearrange("p a t -> p (a t)"), ps[0:rows, bank, :],
                                   ACT.Copy, scale=qk_gain[0:rows, B.layer, unit:unit + 1]).then_inc(qky_done, 1)
                else:
                    act.activation(qk_y[0:rows, 2, 0, :], ps[0:rows, bank, 0:TOK], ACT.Copy,
                                   scale=qk_gain[0:rows, B.layer, 0:1])
                    act.activation(qk_y[0:rows, 2, 1, :], ps[0:rows, bank, TOK:2 * TOK], ACT.Copy,
                                   scale=qk_gain[0:rows, B.layer, 1:2]).then_inc(qky_done, 1)

            def negate_max(B, half):
                act.wait_ge(maxt_ps, (B.n - NB) * 2 + (half + 1))
                wait(act, maxrow_in[half], B.n * 16)
                act.activation(negmax[:, half, :], ps[0:8, BANK_C, 0:TOK], ACT.Copy, scale=-1.0
                               ).then_inc(negmax_done, 1)

            def negate_max_tok(B):
                act.wait_ge(max_done, B.n * H + H)
                for half in range(2):
                    wait(act, maxrow_in[half], B.n * 16)
                act.activation(negmax_tok[:, :], mx_tok[:, :], ACT.Copy, scale=-1.0).then_inc(negmax_done, 2)

            def exps_tok(B, e):
                act.wait_ge(st_ps, B.n * H + 2 * e + 2)
                wait(act, av_ps, B.n * NG + (e // 2 - 1))
                act.activation(prob[:, e % 4 * 2:e % 4 * 2 + 2, 0, :],
                               ps[:, BANK_ST[e % 2], :].rearrange("p (a t) -> p a t", a=2), ACT.Exp
                               ).then_inc(exp_done, 2)

            def exps(B, h):
                act.wait_ge(st_ps, B.n * H + (h + 1))
                g = h // GH
                wait(act, av_ps, B.n * NG + (g - 1))
                act.activation(prob[:, h % (2 * GH), :, :].rearrange("p a t -> p (a t)"),
                               ps[:, BANK_ST[h % 2], :], ACT.Exp).then_inc(exp_done, 1)

            def o_copy(B, g):
                act.wait_ge(av_ps, B.n * NG + (g + 1))
                wait(act, oy_done, B.n * NG + (g - 1))
                act.activation(o_sb[:, g % 2, :], ps[:, BANK_AV, 0:TOK], ACT.Copy).then_inc(o_done, 1)

            def reciprocals(B, g):
                act.wait_ge(sum_ps, B.n * NG + (g + 1))
                wait(act, recip_done, B.n * NG + g)
                act.activation(lnsum[:, :], ps[:, BANK_C, 0:TOK], ACT.Ln).then_inc(ln_done, 1)
                act.wait_ge(ln_done, B.n * NG + (g + 1))
                wait(act, oy_done, B.n * NG + (g - 1))
                act.activation(recip[:, g % 2, :], lnsum[:, :], ACT.Exp, scale=-1.0).then_inc(recip_done, 1)

            def attention(layer):
                def step(k, i):
                    a, b, c, t_ = (Batch(layer, k, i + o) for o in (2, 1, 0, -1))
                    has_a, has_b, has_c, has_t = i + 2 <= 7, 0 <= i + 1 <= 7, 0 <= i <= 7, i >= 1
                    act.preload_act_table_set(LN_SET)
                    for s in range(SLOTS):
                        if has_c and layer == 0 and s % 2 == 0:
                            exps_tok(c, s // 2)
                        if has_c and layer == 1:
                            exps(c, s)
                        if has_t and s == 0:
                            o_copy(t_, 3)
                        if has_t and s == 1:
                            reciprocals(t_, 3)
                        if has_a:
                            if s == 3:
                                modulate(a, 0)
                            if s == 5:
                                qk_out(a, 0, 0)
                                qk_out(a, 0, 1)
                            if s == 6:
                                qk_out(a, 1, 0)
                                if layer == 1:
                                    squares(a, 0)
                            if s == 7:
                                qk_out(a, 1, 1)
                                if layer == 1:
                                    squares(a, 1)
                            first = 9 if layer == 0 else 11
                            if s in (first, first + 1, first + 2):
                                heads_out(a, s - first)
                        if has_c and s in (5, 9, 13):
                            o_copy(c, (s - 5) // 4)
                        if has_c and s in (6, 10, 14):
                            reciprocals(c, (s - 6) // 4)
                        if has_b and layer == 0 and s == 15:
                            negate_max_tok(b)
                        if has_b and layer == 1 and s == 11:
                            negate_max(b, 0)
                        if has_b and layer == 1 and s == 15:
                            negate_max(b, 1)
                attention_steps(act, step)

            def gelus(B, m):
                j = m // 3
                act.wait_ge(f1_ps, B.n * NM + (m + 1))
                if m % 3 == 0:
                    wait(act, glo_done, B.n * 3 + (j - 1))
                func = ACT.Gelu if B.layer == 0 else ACT.Gelu_apprx_tanh
                act.activation(g_y[:, (B.par + j) % 2, m % 3, :], ps[:, BANK_F1[m % 3], 0:TOK], func
                               ).then_inc(gelu_done, 1)

            def mlp(layer):
                def step(k, i):
                    d, e = Batch(layer, k, i + 2), Batch(layer, k, i + 1)
                    if i + 2 <= 7:
                        modulate(d, 1)
                    if i == -2:
                        split_hi(layer, 1)
                    if i == -1:
                        act.wait_ge(x_att, NT * NB * (layer + 1) + FREE)
                    if 0 <= i + 1 <= 7:
                        for m in range(NM):
                            gelus(e, m)
                mlp_steps(act, step)

            act.wait_ge(ada_in, 16)
            act.activation(c_e[:, :, :], c_t[:, :, :], ACT.Exp, scale=-1.0).then_inc(c_chain, 1)
            split_hi(0, 0)
            act.wait_ge(ada_rowed, 8)
            gates = ada_row[:, 4 * ADA_KIND:ADA]
            act.activation(gates, gates, ACT.Tanh).then_inc(tanh_done, 1)
            act.wait_ge(gates_out, 32)
            for layer in range(2):
                if layer == 1:
                    split_hi(1, 0)
                    act.wait_ge(x_mlp, NT * NB)
                attention(layer)
                mlp(layer)

        @block.vector
        def _(dve):
            def split_lo(layer, phase):
                for c, (src, hi, lo) in enumerate(chunks(layer, phase)):
                    k = chunk_base(layer, phase) + c
                    dve.wait_ge(w_hi, k + 1)
                    raw = stage[:, k % 2, 0:src.shape[1]]
                    if lo is not None:
                        dve.tensor_tensor(lo, raw, hi.bitcast(F32), ALU.subtract).then_inc(w_lo, 1)
                    else:
                        dve.scalar_tensor_tensor(out=hi, in0=hi.bitcast(F32), scalar=mask_w[:, 0:1], in1=raw,
                                                 op0=ALU.mult, op1=ALU.add).then_inc(w_lo, 1)

            def stats(B, phase):
                q = q_of(B, phase)
                if phase == 1:
                    dve.wait_ge(x_att, (B.n + 1) * NT + FREE)
                elif B.layer == 1:
                    dve.wait_ge(x_mlp, (B.n - NB + 1) * NT)
                for t in range(NT):
                    dve.bn_stats(bn[:, t, :], x_sb[:, B.pair, B.par, t, :]).then_inc(bn_done, 1)
                wait(dve, rstd_done, q)
                wait(dve, bn_done, (q + 1) * NT)
                dve.memset(waits[:, :], 0.0)
                for t in range(NT):
                    dve.bn_aggr(mv[:, t, :], bn[:, t, :]).then_inc(stats_done, 1)

            def normalize(B, phase):
                q = q_of(B, phase)
                dve.wait_ge(rstd_done, q + 1)
                dve.wait_ge(stats_done, (q + 1) * NT)
                wait(dve, zt_ps, q * 2)
                for t in range(NT):
                    xt = x_sb[:, B.pair, B.par, t, :]
                    rest = z[:, t, 2 * P:].rearrange("p (a r) -> p a r", a=3)
                    wide = xt[:, 2 * P:].unsqueeze(1).to_broadcast([P, 3, REM])
                    for o, x_in in ((z[:, t, 0:2 * P], xt[:, 0:2 * P]), (rest, wide)):
                        if B.layer == 0:
                            ins = dve.tensor_scalar(o, x_in, mv[:, t, 0:1], rstd[:, t:t + 1], ALU.subtract, ALU.mult)
                        else:
                            ins = dve.tensor_scalar(o, x_in, rstd[:, t:t + 1], None, ALU.mult)
                        ins.then_inc(z_done, 1)

            def h_hi(B, phase):
                q = q_of(B, phase)
                dve.wait_ge(y_done, (q + 1) * 3)
                dve.tensor_copy(hs[:, B.par, 0:3, :], y[:, :, :]).then_inc(hs_hi, 1)
                dve.wait_ge(hs_hi, q + 1)
                rem = hs[:, B.par, 2, :]
                dve.scalar_tensor_tensor(out=rem, in0=rem.bitcast(F32), scalar=mask_x[:, 0:1], in1=y[:, 2, :],
                                         op0=ALU.mult, op1=ALU.add).then_inc(hs_rem, 1)

            def v_out(B, t):
                dve.wait_ge(v_ps, B.n * NT + (t + 1))
                wait(dve, av_ps, B.n * NG - NG if isinstance(B.n, int) else B.n * NG + (-NG))
                if B.layer == 0:
                    wait(dve, vrow_out, B.n * 16)
                    dve.tensor_copy(v_rows[:, t, :], ps[:, BANK_A[t], 0:D]).then_inc(v_done, 1)
                    return
                dve.tensor_copy(v_sb[:, B.par, t, :, 0:DH],
                                ps[:, BANK_A[t], 0:D].rearrange("p (h d) -> p h d", h=H)).then_inc(v_done, 1)

            def head_sums(B, t):
                m = B.n - NB
                dve.wait_ge(sq_done, m * NT + (t + 1))
                if t == 0:
                    wait(dve, norm_done, m * NT)
                for side in range(2):
                    dve.tensor_reduce(ss[:, t, side * H:side * H + 2 * BH].rearrange("p (b h) -> p b h", b=2),
                                      sq[:, side * D:side * D + 2 * BLK].rearrange("p (b d h) -> p b h d", b=2, d=DH),
                                      AX.X, ALU.add)
                    last = dve.tensor_reduce(ss[:, t, side * H + 2 * BH:(side + 1) * H],
                                             sq[:, side * D + 2 * BLK:(side + 1) * D].rearrange("p (d h) -> p h d", d=DH),
                                             AX.X, ALU.add)
                last.then_inc(ss_done, 1)

            def rsqrt_heads(B):
                m = B.n - NB
                dve.wait_ge(ss_done, (m + 1) * NT)
                chain = [0]

                def link(ins):
                    chain[0] += 1
                    ins.then_inc(rs_chain, 1)
                    dve.wait_ge(rs_chain, m * 12 + chain[0])

                link(dve.tensor_scalar(ss[:, :, :], ss[:, :, :], EPS1 * EPS1, None, ALU.max))
                link(dve.tensor_scalar(rt[:, :, :].bitcast(U32), ss[:, :, :].bitcast(U32), 1, None,
                                       ALU.logical_shift_right))
                link(dve.tensor_scalar(rs[:, :, :].bitcast(I32), rt[:, :, :].bitcast(I32), -1.0, float(0x5F3759DF),
                                       ALU.mult, ALU.add))
                for _ in range(3):
                    link(dve.tensor_tensor(rt[:, :, :], rs[:, :, :], ss[:, :, :], ALU.mult))
                    link(dve.scalar_tensor_tensor(out=rt[:, :, :], in0=rt[:, :, :], scalar=-0.5, in1=rs[:, :, :],
                                                  op0=ALU.mult, op1=ALU.mult))
                    link(dve.scalar_tensor_tensor(out=rs[:, :, :], in0=rt[:, :, :], scalar=1.5, in1=rs[:, :, :],
                                                  op0=ALU.add, op1=ALU.mult))

            def qk_high(B, unit):
                rows = BLK
                dve.wait_ge(qky_done, B.n * 3 + (unit + 1))
                if unit == 0:
                    first = isinstance(B.n, int) and B.n == 0
                    if not first:
                        other = 1 - B.par
                        dve.wait_ge(stack_in[other], stack_count(B, -1))
                dve.tensor_copy(qk_hi[0:rows, unit, :, :], qk_y[0:rows, unit, :, :]).then_inc(qkhi_done, 1)

            def head_max(B, h):
                dve.wait_ge(max_ps, B.n * H + (h + 1))
                if h == 0:
                    wait(dve, maxt_ps, (B.n - NB) * 2)
                dve.tensor_reduce(mx[:, :, h], ps[:, BANK_MAX[h % 2], :].rearrange("p (a t) -> p a t", a=NT),
                                  AX.X, ALU.max).then_inc(max_done, 1)

            def group_max(B, e):
                dve.wait_ge(max_ps, B.n * H + 2 * e + 2)
                if e == 0:
                    wait(dve, negmax_done, B.n * 2)
                g = token_group(e // 2, e % 2, 0)
                dve.tensor_reduce(mx_tok[:, g:g + GH], ps[:, BANK_MAX[e % 2], :].rearrange("p (a t) -> p a t", a=GH),
                                  AX.X, ALU.max).then_inc(max_done, 2)

            def divide(B, g):
                G = B.n * NG
                dve.wait_ge(recip_done, G + (g + 1))
                wait(dve, olo_done, G + (g - 1))
                dve.tensor_tensor(o_y[:, g % 2, :], o_sb[:, g % 2, :], recip[:, g % 2, :], ALU.mult).then_inc(oy_done, 1)
                dve.wait_ge(oy_done, G + (g + 1))
                if g == 0:
                    wait(dve, proj_ps, B.n * NT)
                dve.tensor_copy(o_hi[:, g, :], o_y[:, g % 2, :]).then_inc(ohi_done, 1)

            def gated(B, t):
                dve.wait_ge(proj_ps, B.n * NT + (t + 1))
                if t == 0:
                    dve.wait_ge(gate_in[B.par], gate_count(B, 0))
                if B.layer == 1 and isinstance(B.b, int) and B.b == 0:
                    dve.wait_ge(x_mlp, NT * NB)
                dve.wait_ge(x_att, B.n * NT + (t + 1 - NT + FREE))
                dve.tensor_tensor(res[:, t, :], ps[:, BANK_C, 0:D], gate[:, B.par, :], ALU.mult).then_inc(res_done, 1)

            def attention(layer):
                def step(k, i):
                    a, b, c, t_ = (Batch(layer, k, i + o) for o in (2, 1, 0, -1))
                    has_a, has_b, has_c, has_t = i + 2 <= 7, 0 <= i + 1 <= 7, 0 <= i <= 7, i >= 1
                    for s in range(SLOTS):
                        if has_a and s == 0:
                            if layer == 0 and i == 0:
                                dve.wait_ge(x_rest, 16 * (NB // 2 - 1))
                            stats(a, 0)
                        if has_a and s == 1:
                            normalize(a, 0)
                        if has_t and s == 2:
                            divide(t_, 3)
                        if has_a and s == 3:
                            h_hi(a, 0)
                        if has_t and s in (5, 6):
                            gated(t_, s - 5)
                        if has_b and s in (1, 2):
                            v_out(b, s - 1)
                        if has_c and s in (7, 11, 15):
                            divide(c, (s - 7) // 4)
                        if has_a and layer == 1 and s in (7, 8):
                            head_sums(a, s - 7)
                        if has_a and layer == 1 and s == 8:
                            rsqrt_heads(a)
                        first = 10 if layer == 0 else 12
                        if has_a and s in (first, first + 1, first + 2):
                            qk_high(a, s - first)
                        if has_b:
                            for h in max_heads(s):
                                if layer == 1:
                                    head_max(b, h)
                                elif h % 2:
                                    group_max(b, h // 2)
                attention_steps(dve, step)

            def g_high(B, j):
                dve.wait_ge(gelu_done, B.n * NM + 3 * (j + 1))
                if j == 0:
                    wait(dve, f2_ps, B.n * NT - NT if isinstance(B.n, int) else B.n * NT + (-NT))
                par = (B.par + j) % 2
                dve.tensor_copy(g_hi[:, B.par, 3 * j:3 * j + 3, :], g_y[:, par, :, :]).then_inc(ghi_done, 1)

            def bias_gate(B, t):
                dve.wait_ge(f2_ps, B.n * NT + (t + 1))
                if t == 0:
                    dve.wait_ge(gate_in[B.par], gate_count(B, 1))
                if t == 0:
                    dve.wait_ge(b2_in, 16 * (B.layer + 1))
                    dve.wait_ge(x_att, NT * NB * (B.layer + 1) + FREE)
                wait(dve, x_mlp, B.n * NT - NT + t + 1 if isinstance(B.n, int) else B.n * NT + (t + 1 - NT))
                dve.tensor_tensor(res[:, t, :], ps[:, BANK_F2[t], 0:D], b2[:, :], ALU.add).then_inc(f2b_done, 1)
                dve.wait_ge(f2b_done, B.n * NT + (t + 1))
                dve.tensor_tensor(res[:, t, :], res[:, t, :], gate[:, B.par, :], ALU.mult).then_inc(f2g_done, 1)

            def mlp(layer):
                def step(k, i):
                    d, e, f = Batch(layer, k, i + 2), Batch(layer, k, i + 1), Batch(layer, k, i)
                    if i + 2 <= 7:
                        stats(d, 1)
                        normalize(d, 1)
                        h_hi(d, 1)
                    if i == -2:
                        split_lo(layer, 1)
                    if 0 <= i + 1 <= 7:
                        g_high(e, 0)
                        g_high(e, 1)
                    if 0 <= i:
                        bias_gate(f, 0)
                    if 0 <= i + 1 <= 7:
                        g_high(e, 2)
                    if 0 <= i:
                        bias_gate(f, 1)
                mlp_steps(dve, step)

            dve.memset(y[:, 2, :], 1.0).then_inc(gain_set, 1)
            dve.memset(qk_gain[:, 0, 0:1], float(DH) ** -0.5)
            dve.memset(qk_gain[:, 0, 1:2], 1.0).then_inc(gain_set, 1)
            dve.wait_ge(const_in, 16 * 7)
            dve.tensor_copy(apart_r[:, :, :], apart[:, :, :]).then_inc(apart_rounded, 1)
            dve.tensor_copy(qk_gain[:, 1, 0:1], gains[:, 2:3])
            dve.tensor_scalar(qk_gain[:, 1, 1:2], gains[:, 3:4], float(DH) ** 0.5, None, ALU.mult).then_inc(gain_set, 1)
            dve.wait_ge(c_chain, 1)
            dve.tensor_scalar(c_e[:, :, :], c_e[:, :, :], 1.0, None, ALU.add).then_inc(c_chain, 1)
            dve.wait_ge(c_chain, 2)
            dve.reciprocal(c_e[:, :, :], c_e[:, :, :]).then_inc(c_chain, 1)
            dve.wait_ge(c_chain, 3)
            dve.tensor_tensor(s_c[:, :, :], c_e[:, :, :], c_t[:, :, :], ALU.mult).then_inc(c_chain, 1)
            split_lo(0, 0)
            for layer in range(2):
                for c in range(4):
                    w = ADA // 4
                    dve.wait_ge(ada_ps, 4 * layer + c + 1)
                    if layer == 1 and c == 0:
                        dve.wait_ge(gates_out, 16)
                        dve.wait_ge(ada_tr, 1)
                    dve.tensor_tensor(ada_row[:, c * w:(c + 1) * w], ps[0:NB, 4 * layer + c, 0:w],
                                      ada_b[:, layer, c * w:(c + 1) * w], ALU.add).then_inc(ada_rowed, 1)
                dve.wait_ge(ada_tr, layer + 1)
                for kind in range(4):
                    for blk in range(3):
                        rows = P if blk < 2 else 3 * REM
                        o = mod[0:rows, layer, kind, blk, :, :].rearrange("p k a -> p (k a)")
                        at = (kind * 3 + blk) * NB
                        src = ps[0:rows, 4 * layer, at:at + NB]
                        if kind % 2 == 0:
                            ins = dve.tensor_copy(o, src)
                        elif layer == 0:
                            ins = dve.tensor_scalar(o, src, 1.0, None, ALU.add)
                        else:
                            ins = dve.tensor_scalar(o, src, 1.0, gains[0:rows, kind // 2:kind // 2 + 1], ALU.add, ALU.mult)
                ins.then_inc(mod_set, 1)
            dve.wait_ge(gates_out, 32)
            for layer in range(2):
                if layer == 1:
                    split_lo(1, 0)
                    dve.wait_ge(x_mlp, NT * NB)
                dve.memset(v_sb[:, :, :, :, DH + 1:32].rearrange("p a t h e -> p (a t h) e"), 0.0)
                dve.memset(v_sb[:, :, :, :, DH:DH + 1].rearrange("p a t h e -> p (a t h) e"), 1.0).then_inc(v_ones, 1)
                if layer == 0:
                    dve.wait_ge(x_first, 16)
                attention(layer)
                mlp(layer)

        @block.tensor
        def _(pe):
            def transpose_z(B, phase):
                q = q_of(B, phase)
                pe.wait_ge(z_done, q * 4 + 4)
                if phase == 0 and not B.first:
                    pe.wait_ge(v_done, B.n * NT)
                wait(pe, y_done, q * 3)
                for blk in range(2):
                    for t in range(NT):
                        ins = pe.transpose(ps[:, BANK_A[0], blk * TOK + t * P:blk * TOK + (t + 1) * P],
                                           z[:, t, blk * P:(blk + 1) * P], ident[:, :])
                ins.then_inc(zt_ps, 1)
                for t in range(NT):
                    ins = pe.transpose(ps[0:3 * REM, BANK_A[1], t * P:(t + 1) * P], z[:, t, 2 * P:], ident[:, :])
                ins.then_inc(zt_ps, 1)

            def rows_product(bank, B, t, w, cols):
                tok = slice(t * P, (t + 1) * P)
                passes = [(0, 0, P), (1, 1, P), (0, 3, P), (1, 4, P), (3, 0, P), (4, 1, P), (2, 2, KREM)]
                for n, (a, b, rows) in enumerate(passes):
                    ins = pe.matmul(ps[:, bank, 0:D], hs[0:rows, B.par, a, tok], w[0:rows, b, cols],
                                    start=(n == 0), stop=(n == len(passes) - 1))
                return ins

            def qk(B, t, part):
                n = B.n
                if t == 0 and part == 0:
                    pe.wait_ge(hs_rem, B.qa + 1)
                    pe.wait_ge(hs_lo, B.qa + 1)
                if t == 1:
                    pe.wait_ge(row_done, n * 4 + (part + 1))
                rows_product(BANK_A[part], B, t, wqkv, slice(part * D, (part + 1) * D)).then_inc(qk_ps, 1)

            def v_product(B, t):
                pe.wait_ge(qky_done, B.n * 3 + 3)
                rows_product(BANK_A[t], B, t, wqkv, slice(2 * D, 3 * D)).then_inc(v_ps, 1)

            def heads_transpose(B, unit):
                n = B.n
                if unit == 0:
                    if B.layer == 0:
                        pe.wait_ge(row_done, n * 4 + 4)
                    else:
                        pe.wait_ge(norm_done, (n - NB) * NT + NT)
                        pe.wait_ge(row_done, n * 4 + 4)
                elif unit == 2:
                    wait(pe, qky_done, n * 3 + 1)
                bank = BANK_A[unit % 2]
                for half in range(2):
                    if unit < 2:
                        lo, rows = unit * D + half * BLK, BLK
                    else:
                        lo, rows = (half + 1) * D - BLK, BLK
                    for t in range(NT):
                        ins = pe.transpose(ps[0:rows, bank, half * TOK + t * P:half * TOK + (t + 1) * P],
                                           qk_row[:, t, lo:lo + rows], ident[:, :])
                ins.then_inc(qkt_ps, 1)

            def max_scores(B, h):
                if h == 0:
                    pe.wait_ge(stack_in[B.par], stack_count(B, 0))
                wait(pe, max_done, B.n * H + (h - 1))
                q, k = stack[0:KSUM, B.par, 0, h, :], stack[0:KSUM, B.par, 1, h, :]
                for t in range(NT):
                    ins = pe.matmul(ps[:, BANK_MAX[h % 2], t * TOK:(t + 1) * TOK], q[:, t * P:(t + 1) * P], k,
                                    start=True, stop=True)
                ins.then_inc(max_ps, 1)

            def max_scores_tok(B, e):
                if e == 0:
                    pe.wait_ge(stack_in[B.par], stack_count(B, 0))
                wait(pe, max_done, B.n * H + 2 * e - 2)
                for c in range(GH):
                    g = token_group(e // 2, e % 2, c)
                    ins = pe.matmul(ps[:, BANK_MAX[e % 2], c * P:(c + 1) * P], by_group(KSUM, B.par, 0, g),
                                    by_group(KSUM, B.par, 1, g), start=True, stop=True)
                ins.then_inc(max_ps, 2)

            def scores_tok(B, e):
                if e == 0:
                    for half in range(2):
                        pe.wait_ge(maxrow_in[half], B.n * 16 + 16)
                wait(pe, exp_done, B.n * H + 2 * e - 2)
                for c in range(GH):
                    g = token_group(e // 2, e % 2, c)
                    ins = pe.matmul(ps[:, BANK_ST[e % 2], c * P:(c + 1) * P], by_group(KSUM + 1, B.par, 1, g),
                                    by_group(KSUM + 1, B.par, 0, g), start=True, stop=True)
                ins.then_inc(st_ps, 2)

            def prob_v_tok(B, u):
                pe.wait_ge(exp_done, B.n * H + GH * (u + 1))
                wait(pe, o_done, B.n * NG + u)
                if u == 0:
                    pe.wait_ge(v_in[B.par], 16 * B.pair + 16)
                for half in range(2):
                    e = 2 * u + half
                    p4 = prob[:, e % 4 * 2:e % 4 * 2 + 2, 0, :]
                    for c in range(GH):
                        ins = pe.matmul(ps[32 * c:32 * c + 32, BANK_AV, half:TOK:2],
                                        v_group[:, B.par, token_group(u, half, c), :],
                                        p4[:, c // 2, c % 2 * P:(c % 2 + 1) * P], start=True, stop=True)
                ins.then_inc(av_ps, 1)

            def transpose_max(B, half, has_c, c):
                pe.wait_ge(max_done, B.n * H + 8 * (half + 1))
                if has_c:
                    pe.wait_ge(ln_done, c.n * NG + (2 + half))
                elif half == 1:
                    pe.wait_ge(negmax_done, B.n * 2 + 1)
                for t in range(NT):
                    ins = pe.transpose(ps[0:8, BANK_C, t * P:(t + 1) * P], mx[:, t, 8 * half:8 * half + 8], ident[:, :])
                ins.then_inc(maxt_ps, 1)

            def scores(B, h):
                if h % 8 == 0:
                    pe.wait_ge(maxrow_in[h // 8], B.n * 16 + 16)
                wait(pe, exp_done, B.n * H + (h - 1))
                q, k = stack[0:KSUM + 1, B.par, 0, h, :], stack[0:KSUM + 1, B.par, 1, h, :]
                for t in range(NT):
                    ins = pe.matmul(ps[:, BANK_ST[h % 2], t * TOK:(t + 1) * TOK], k[:, t * P:(t + 1) * P], q,
                                    start=True, stop=True)
                ins.then_inc(st_ps, 1)

            def prob_v(B, g):
                pe.wait_ge(exp_done, B.n * H + GH * (g + 1))
                wait(pe, o_done, B.n * NG + g)
                if g == 0:
                    pe.wait_ge(v_done, B.n * 2 + 2)
                for t in range(NT):
                    for j in range(GH):
                        h = GH * g + j
                        ins = pe.matmul(ps[32 * j:32 * j + 32, BANK_AV, 0:TOK], v_sb[:, B.par, t, h, :],
                                        prob[:, h % (2 * GH), t, :], start=(t == 0), stop=(t == NT - 1))
                ins.then_inc(av_ps, 1)

            def spread_sums(B, g):
                pe.wait_ge(o_done, B.n * NG + (g + 1))
                pe.matmul(ps[:, BANK_C, 0:TOK], sumsel[:, :], o_sb[:, g % 2, :], start=True, stop=True).then_inc(sum_ps, 1)

            def project(B, t):
                if t == 0:
                    pe.wait_ge(ohi_done, (B.n + 1) * NG)
                    pe.wait_ge(olo_done, (B.n + 1) * NG)
                    pe.wait_ge(ln_done, (B.n + 1) * NG)
                else:
                    pe.wait_ge(res_done, B.n * NT + 1)
                tok, n = slice(t * P, (t + 1) * P), 0
                for g in range(NG):
                    for o, w in ((o_hi, 0), (o_hi, 1), (o_lo, 0)):
                        ins = pe.matmul(ps[:, BANK_C, 0:D], o[:, g, tok], wproj[:, w, g, :],
                                        start=(n == 0), stop=(n == 3 * NG - 1))
                        n += 1
                ins.then_inc(proj_ps, 1)

            def attention(layer):
                def step(k, i):
                    a, b, c, t_ = (Batch(layer, k, i + o) for o in (2, 1, 0, -1))
                    has_a, has_b, has_c, has_t = i + 2 <= 7, 0 <= i + 1 <= 7, 0 <= i <= 7, i >= 1
                    for s in range(SLOTS):
                        tok = layer == 0
                        if has_c and not tok:
                            scores(c, s)
                        if has_c and tok and s % 2 == 0:
                            scores_tok(c, s // 2)
                        if has_t and s == 0:
                            (prob_v_tok if tok else prob_v)(t_, 3)
                        if has_t and s == 1:
                            if has_c and not tok:
                                pe.wait_ge(negmax_done, c.n * 2 + 2)
                            else:
                                pe.wait_ge(ln_done, t_.n * NG + 3)
                            spread_sums(t_, 3)
                        if has_a and s == 2:
                            transpose_z(a, 0)
                        if has_t and s in (4, 5):
                            project(t_, s - 4)
                        if has_c and s in (5, 9, 13):
                            (prob_v_tok if tok else prob_v)(c, (s - 5) // 4)
                        if has_a and s in (5, 6):
                            qk(a, s - 5, 0)
                            qk(a, s - 5, 1)
                        if has_b and s == 1:
                            v_product(b, 0)
                            v_product(b, 1)
                        if has_c and s == 6:
                            if has_t:
                                pe.wait_ge(res_done, (t_.n + 1) * NT)
                            elif not tok:
                                pe.wait_ge(negmax_done, c.n * 2 + 2)
                            spread_sums(c, 0)
                        if has_c and s == 10:
                            pe.wait_ge(ln_done, c.n * NG + 1)
                            spread_sums(c, 1)
                        if has_c and s == 14:
                            if has_b and not tok:
                                pe.wait_ge(negmax_done, b.n * 2 + 1)
                            else:
                                pe.wait_ge(ln_done, c.n * NG + 2)
                            spread_sums(c, 2)
                        first = 9 if layer == 0 else 11
                        if has_a and s in (first, first + 1, first + 2):
                            heads_transpose(a, s - first)
                        if has_b:
                            for h in max_heads(s):
                                if not tok:
                                    max_scores(b, h)
                                elif h % 2:
                                    max_scores_tok(b, h // 2)
                        if has_b and not tok and s == 11:
                            transpose_max(b, 0, has_c, c)
                        if has_b and not tok and s == 15:
                            transpose_max(b, 1, has_c, c)
                attention_steps(pe, step)

            def fc1(B, m):
                if m == 0:
                    pe.wait_ge(hs_rem, B.qm + 1)
                    pe.wait_ge(hs_lo, B.qm + 1)
                wait(pe, gelu_done, B.n * NM + (m - 2))
                cols = slice(m * P, (m + 1) * P)
                passes = [(0, 0, P), (1, 1, P), (0, 3, P), (1, 4, P), (3, 0, P), (4, 1, P), (2, 2, KREM)]
                for n, (a, b, rows) in enumerate(passes):
                    ins = pe.matmul(ps[:, BANK_F1[m % 3], 0:TOK], w1[0:rows, b, cols], hs[0:rows, B.par, a, :],
                                    start=(n == 0), stop=(n == len(passes) - 1))
                ins.then_inc(f1_ps, 1)

            def fc2(B, t):
                if t == 0:
                    pe.wait_ge(ghi_done, B.n * 3 + 3)
                    pe.wait_ge(glo_done, B.n * 3 + 3)
                wait(pe, f2b_done, B.n * NT - NT + t + 1 if isinstance(B.n, int) else B.n * NT + (t + 1 - NT))
                tok, n = slice(t * P, (t + 1) * P), 0
                for m in range(NM):
                    for g, w in ((g_hi, 0), (g_hi, 1), (g_lo, 0)):
                        ins = pe.matmul(ps[:, BANK_F2[t], 0:D], g[:, B.par, m, tok], w2[:, w, m, :],
                                        start=(n == 0), stop=(n == 3 * NM - 1))
                        n += 1
                ins.then_inc(f2_ps, 1)

            def mlp(layer):
                def step(k, i):
                    d, e, f = Batch(layer, k, i + 2), Batch(layer, k, i + 1), Batch(layer, k, i)
                    if i + 2 <= 7:
                        transpose_z(d, 1)
                    if i == -1:
                        pe.wait_ge(w_lo, chunk_end(layer, 1))
                    if 0 <= i + 1 <= 7:
                        for m in range(5):
                            fc1(e, m)
                    if 0 <= i:
                        fc2(f, 0)
                    if 0 <= i + 1 <= 7:
                        for m in range(5, NM):
                            fc1(e, m)
                    if 0 <= i:
                        fc2(f, 1)
                mlp_steps(pe, step)

            pe.wait_ge(c_chain, 4)
            for layer in range(2):
                pe.wait_ge(ada_w_in, 16 * (layer + 1))
                w = ADA // 4
                for c in range(4):
                    for blk in range(3):
                        rows = P if blk < 2 else REM
                        ins = pe.matmul(ps[0:NB, 4 * layer + c, 0:w], s_c[0:rows, blk, :],
                                        ada_w[0:rows, blk, c * w:(c + 1) * w], start=(blk == 0), stop=(blk == 2))
                    ins.then_inc(ada_ps, 1)
                pe.wait_ge(ada_rowed, 4 * layer + 4)
                pe.wait_ge(const_in, 16 * 7)
                for kind in range(4):
                    for blk in range(3):
                        rows = P if blk < 2 else 3 * REM
                        lo, at = kind * ADA_KIND + blk * P, (kind * 3 + blk) * NB
                        ins = pe.transpose(ps[0:rows, 4 * layer, at:at + NB], ada_row[:, lo:lo + rows],
                                           ident[0:NB, 0:NB])
                ins.then_inc(ada_tr, 1)
            pe.wait_ge(mod_set, 2)
            for layer in range(2):
                pe.wait_ge(w_lo, chunk_end(layer, 0))
                pe.wait_ge(v_ones, layer + 1)
                if layer == 0:
                    pe.wait_ge(mask_in, 16 * 4)
                if layer == 1:
                    pe.wait_ge(f2b_done, NT * NB)
                attention(layer)
                pe.wait_ge(res_done, NT * NB * (layer + 1))
                mlp(layer)


def kernel(**inputs):
    import concourse.bacc as bacc
    from concourse.bass_utils import run_bass_kernel_spmd as run

    a = {k: np.asarray(v) for k, v in inputs.items()}
    f32 = np.float32

    def blocks(w):
        t = np.zeros((P, 3, w.shape[1]), f32)
        t[:, 0], t[:, 1] = w[0:P], w[P:2 * P]
        for r in range(3):
            t[REM * r:REM * (r + 1), 2] = w[2 * P:]
        return t

    order = [h * DH + d for blk in (range(0, BH), range(BH, 2 * BH), range(2 * BH, H)) for d in range(DH) for h in blk]
    cols = np.array(order + [D + o for o in order] + list(range(2 * D, 3 * D)))
    kinds = (0, 1, 3, 4)
    ada_cols = [j for kind in kinds for j in list(range(kind * D, (kind + 1) * D)) + list(range(kind * D + 2 * P, (kind + 1) * D)) * 2]
    ada_cols = np.array(ada_cols + list(range(2 * D, 3 * D)) + list(range(5 * D, 6 * D)))

    ins = {"x": np.ascontiguousarray(a["x"])}
    ada_b = np.zeros((NB, 2, ADA), f32)
    for layer in range(2):
        g = lambda name: a[f"L{layer}_cond_{name}"]
        turn = (lambda w: w) if layer == 0 else (lambda w: w.T)
        wqkv = blocks(turn(g("qkv_w"))[:, cols])
        wqkv[3 * REM:KREM, 2] = g("qkv_b")[cols]
        w1 = blocks(turn(g("fc1_w")))
        w1[3 * REM:KREM, 2] = g("fc1_b")
        wproj = np.zeros((P, NG, D), f32)
        pw = turn(g("proj_w")).reshape(NG, GH, DH, D)
        for j in range(GH):
            wproj[32 * j:32 * j + DH] = pw[:, j].transpose(1, 0, 2)
        wproj[DH, 0] = g("proj_b")
        ins[f"wqkv{layer}"], ins[f"w1{layer}"], ins[f"wproj{layer}"] = wqkv, w1, wproj
        ins[f"w2{layer}"] = np.ascontiguousarray(turn(g("fc2_w")).reshape(NM, P, D).transpose(1, 0, 2))
        ins[f"b2{layer}"] = np.ascontiguousarray(np.broadcast_to(g("fc2_b"), (P, D)))
        ada = np.zeros((P, 3, ADA), f32)
        aw = turn(g("ada_w"))[:, ada_cols]
        ada[:, 0], ada[:, 1], ada[0:REM, 2] = aw[0:P], aw[P:2 * P], aw[2 * P:]
        ins[f"ada_w{layer}"] = ada
        ada_b[:, layer] = g("ada_b")[ada_cols]
    c_t = np.zeros((P, 3, NB), f32)
    ct = a["cond_1152"].T
    c_t[:, 0], c_t[:, 1], c_t[0:REM, 2] = ct[0:P], ct[P:2 * P], ct[2 * P:]
    ins["ada_b"], ins["c_t"] = ada_b, c_t
    own = (np.arange(TG)[:, None] == np.arange(TOK)[None, :] // NGT)
    ins["apart"] = np.ascontiguousarray(np.broadcast_to(
        np.stack([own.astype(f32), np.where(own, 0.0, -BIG).astype(f32)], axis=1), (TG, 2, TOK)))
    ins["ident"] = np.eye(P, dtype=f32)
    rows = np.arange(P)
    ins["sumsel"] = (rows[:, None] == 32 * (rows[None, :] // 32) + DH).astype(f32)
    ins["mask_x"] = -((rows >= 2 * REM) & (rows < 3 * REM)).astype(f32)[:, None]
    ins["mask_w"] = -(((rows >= REM) & (rows < 2 * REM)) | (rows == KREM - 1)).astype(f32)[:, None]
    ins["gains"] = np.ascontiguousarray(np.broadcast_to(
        np.concatenate([a[f"L1_cond_{k}"] for k in ("g1", "g2", "qg", "kg")]), (P, 4)))

    nc = bacc.Bacc("TRN2", target_bir_lowering=False, num_devices=1)
    A = {k: nc.dram_tensor(f"in_{k}", v.shape, F32, kind="ExternalInput").ap() for k, v in ins.items()}
    out = nc.dram_tensor("out", (NB, TOK, D), F32, kind="ExternalOutput").ap()
    build(nc, A, out)
    r = run(nc, [{f"in_{k}": v for k, v in ins.items()}], core_ids=[0])
    return r.results[0]["out"]
```

```python
from contextlib import ExitStack

import numpy as np
import concourse.bass as bass
from concourse import mybir

F32 = mybir.dt.float32
F32R = mybir.dt.float32r
U32 = mybir.dt.uint32
I32 = mybir.dt.int32
ALU = mybir.AluOpType
ACT = mybir.ActivationFunctionType
AX = mybir.AxisListType

P = 128
NB = 8
FREE = 2
TOK = 256
NT = TOK // P
D = 288
H = 16
DH = D // H
F = 4 * D
NM = F // P
REM = D - 2 * P
KREM = 3 * REM + 2
BH = 7
BLK = BH * DH
TAILH = H - 2 * BH
TAIL = BLK - TAILH * DH
KSUM = 96
GH = 4
NG = H // GH
SLOTS = 16
TG = TOK // 32
STAGES = 4
STACK_DMAS = 12
NGT = TOK // TG
MROW = 3 * DH
BIG = 2.0 ** 100
ADA_KIND = 2 * P + 3 * REM
ADA = 4 * ADA_KIND + 2 * D
EPS0 = 1e-6
EPS1 = 1e-12
LN_SET = "natural_log_exp_and_others"

BANK_MAX, BANK_ST, BANK_AV, BANK_A, BANK_C = (0, 1), (2, 3), 4, (5, 6), 7
BANK_F1, BANK_F2 = (0, 1, 2), (3, 4)


def wait(eng, sem, value):
    if isinstance(value, int) and value <= 0:
        return
    eng.wait_ge(sem, value)


def held(eng, value):
    return value if isinstance(value, int) else eng.to_reg(value)


class Batch:

    def __init__(self, layer, pair, offset):
        self.pair, self.par = pair + offset // 2, offset % 2
        self.first = isinstance(self.pair, int) and self.pair == 0 and self.par == 0
        b = self.pair * 2 + self.par
        self.n = b + layer * NB
        self.qa = b + 2 * layer * NB
        self.qm = b + (2 * layer + 1) * NB
        self.layer = layer
        self.b = b


NORM = (1, 1)
Z_T = (8, 5)
SPLIT_H = (12, 9)
QK = ((0, 2), (0, 2))
HEADS_T = (4, 10)
V = (10, 7)
PROJECT = ((0, 2), (9, 13))
W1_SPLIT = 12
MAX_TOK = 2
PROB_V, GROUP_PACE = (3, 5), (2, 4)
O_COPY, SUMS, RECIP, DIVIDE = 1, 2, 3, 4


def groups_at(layer, st, s, after):
    got = []
    for g in range(NG):
        at = PROB_V[layer] + GROUP_PACE[layer] * g + after
        if at == s and st.has_c:
            got.append((st.c, g))
        if at == s + SLOTS and st.has_t:
            got.append((st.t, g))
    return got


def attention_steps(eng, step, first):
    for i in range(first, 1):
        step(0, i)
    with eng.Fori(0, 2) as k:
        for i in (1, 2):
            step(k, i)
    for i in (5, 6, 7):
        step(0, i)


def mlp_steps(eng, step, tail, ahead):
    step(0, -2)
    tail()
    for i in (-1, 0, 1):
        step(0, i)
    with eng.Fori(0, 2) as k:
        for i in (2, 3):
            step(k, i)
    step(0, 6)
    ahead()
    step(0, 7)


def max_heads(s):
    return [h for h in range(H - 3) if 4 + h * 12 // (H - 3) == s]


def late_heads(s):
    return [H - 3 + s] if s < 3 else []


class Stages:

    def __init__(self, layer, k, i):
        self.n, self.a, self.b, self.c, self.t = (Batch(layer, k, i + o) for o in (3, 2, 1, 0, -1))
        self.has_n, self.has_a, self.has_b = i + 3 <= 7, 0 <= i + 2 <= 7, 0 <= i + 1 <= 7
        self.has_c, self.has_t = 0 <= i <= 7, i >= 1


def token_group(u, half, c):
    return 16 * half + GH * u + c


def build(nc, A, out):
    with ExitStack() as ctx:
        sb = lambda name, shape, dt=F32: ctx.enter_context(nc.sbuf_tensor(name, shape, dt))
        sem = lambda name: ctx.enter_context(nc.semaphore(name))

        x_sb = sb("x_sb", [P, NB // 2, 2, NT, D])
        ident = sb("ident", [P, P])
        sumsel = sb("sumsel", [P, P])
        mask_x = sb("mask_x", [P, 1])
        mask_w = sb("mask_w", [P, 1])
        gains = sb("gains", [P, 4])
        qk_gain = sb("qk_gain", [P, 2, 2])
        neg_half = sb("neg_half", [P, NT])
        floor = sb("floor", [P, 2, NT])
        mod = sb("mod", [P, 2, 4, 3, NB // 2, 2])
        s_c = sb("s_c", [P, 3, NB])
        wqkv = sb("wqkv", [P, 5, 3 * D], F32R)
        wproj = sb("wproj", [P, 2, NG, D], F32R)
        waits = sb("waits", [P, 1])
        bn = sb("bn", [P, NT, 6])
        mv = sb("mv", [P, NT, 2])
        vtmp = sb("vtmp", [P, NT])
        vtmp2 = sb("vtmp2", [P, NT])
        rstd = sb("rstd", [P, NT])
        z = sb("z", [P, NT, 2 * P + 3 * REM])
        y = sb("y", [P, 3, TOK])
        hs = sb("hs", [P, 2, 5, TOK], F32R)
        gate = sb("gate", [P, 2, D])
        res = sb("res", [P, NT, D])
        big = sb("big", [P, 2, 2, H * TOK], F32R)
        stack = big[:, :, :, :].rearrange("p a b (h t) -> p a b h t", h=H)
        flat = big[:, :, :, :].rearrange("p a b c -> p (a b c)")
        w1 = flat[:, 0:5 * F].rearrange("p (k n) -> p k n", k=5)
        w2 = flat[:, 5 * F:5 * F + 2 * NM * D].rearrange("p (s m n) -> p s m n", s=2, m=NM)

        with ExitStack() as at:
            sa = lambda name, shape, dt=F32: at.enter_context(nc.sbuf_tensor(name, shape, dt))
            qk_row = sa("qk_row", [P, NT, 2 * D])
            sq = sa("sq", [P, 2 * D])
            ss = sa("ss", [P, NT, 2 * H])
            rs = sa("rs", [P, NT, 2 * H])
            rt = sa("rt", [P, NT, 2 * H])
            qk_y = sa("qk_y", [P, 3, 2, TOK])
            qk_hi = sa("qk_hi", [P, 3, 2, TOK], F32R)
            qk_lo = sa("qk_lo", [P, 3, 2, TOK], F32R)
            prob = sa("prob", [P, 2 * GH, NT, TOK])
            o_sb = sa("o_sb", [P, 2, TOK])
            lnsum = sa("lnsum", [P, TOK])
            recip = sa("recip", [P, 2, TOK])
            o_y = sa("o_y", [P, 2, TOK])
            o_hi = sa("o_hi", [P, 2, NG, TOK], F32R)
            o_lo = sa("o_lo", [P, 2, NG, TOK], F32R)
            v_sb = sa("v_sb", [P, 2, NT, H, 32])
            mx = sa("mx", [P, NT, H])
            negmax = sa("negmax", [8, 2, TOK], F32R)
            mx_tok = sa("mx_tok", [P, NGT])
            negmax_tok = sa("negmax_tok", [P, NGT], F32R)
        with ExitStack() as ml:
            sm = lambda name, shape, dt=F32: ml.enter_context(nc.sbuf_tensor(name, shape, dt))
            stage = sm("stage", [P, STAGES, F])
            b2 = sm("b2", [P, D])
            g_y = sm("g_y", [P, 2, 3, TOK])
            g_hi = sm("g_hi", [P, 2, NM, TOK], F32R)
            g_lo = sm("g_lo", [P, 2, NM, TOK], F32R)
        with ExitStack() as ad:
            sd = lambda name, shape, dt=F32: ad.enter_context(nc.sbuf_tensor(name, shape, dt))
            stage_again = sd("stage_again", [P, STAGES, F])
            apart = sd("apart", [TG, 2, TOK])
            apart_r = sd("apart_r", [TG, 2, TOK], F32R)
            c_e = sd("c_e", [P, 3, NB])
            c_t = sd("c_t", [P, 3, NB])
            sd("gap", [P, (2 * NT * D + 2 * D + 6 * NT * H + 18 * TOK) - STAGES * F - 4 * TOK - 6 * NB])
            ada_w = sd("ada_w", [P, 3, ADA])
            ada_row = sd("ada_row", [NB, ADA])
            ada_b = sd("ada_b", [NB, ADA])


        by_group = lambda rows, par, side, g: big[0:rows, par, side, g::NGT]
        v_rows = sq[:, :].rearrange("p (t d) -> p t d", t=NT)
        v_group = v_sb[:, :, :, :, :].rearrange("p a t h e -> p a (t h) e")
        v_dram = nc.dram_tensor("v_scratch", (2, TOK, D), F32, kind="Internal").ap()
        ps = ctx.enter_context(nc.psum_tensor("ps", [P, 8, 512], F32))
        gates_dram = nc.dram_tensor("gates_scratch", (2, NB, 2, D), F32, kind="Internal").ap()

        x_first, x_rest, const_in, ada_in = sem("x_first"), sem("x_rest"), sem("const_in"), sem("ada_in")
        ada_b_in = sem("ada_b_in")
        ada_w_in, gain_set = sem("ada_w_in"), sem("gain_set")
        const_set, c_chain, v_ones = sem("const_set"), sem("c_chain"), sem("v_ones")
        ada_ps, ada_rowed, ada_tr, mod_set = sem("ada_ps"), sem("ada_rowed"), sem("ada_tr"), sem("mod_set")
        tanh_done, gates_out = sem("tanh_done"), sem("gates_out")
        w_in = [sem(f"w_in{k}") for k in range(STAGES)]
        w_hi, w_lo = sem("w_hi"), sem("w_lo")
        b2_in = sem("b2_in")
        zeroed = sem("zeroed")
        bn_done, stats_done, var_done, rstd_done = sem("bn_done"), sem("stats_done"), sem("var_done"), sem("rstd_done")
        z_done, zt_ps, y_done = sem("z_done"), sem("zt_ps"), sem("y_done")
        hs_hi, hs_rem, hs_lo = sem("hs_hi"), sem("hs_rem"), sem("hs_lo")
        qk_ps, row_done, v_ps, v_done = sem("qk_ps"), sem("row_done"), sem("v_ps"), sem("v_done")
        vrow_out, v_in, mask_in = sem("vrow_out"), [sem("v_in0"), sem("v_in1")], sem("mask_in")
        apart_rounded = sem("apart_rounded")
        sq_done, ss_done, rs_chain, norm_done = sem("sq_done"), sem("ss_done"), sem("rs_chain"), sem("norm_done")
        qkt_ps, qky_done, qkhi_done, qklo_done = sem("qkt_ps"), sem("qky_done"), sem("qkhi_done"), sem("qklo_done")
        stack_in = [sem("stack_in0"), sem("stack_in1")]
        max_ps, max_done, maxt_ps, negmax_done = sem("max_ps"), sem("max_done"), sem("maxt_ps"), sem("negmax_done")
        maxrow_in = [sem("maxrow_in0"), sem("maxrow_in1")]
        st_ps, exp_done, av_ps, o_done = sem("st_ps"), sem("exp_done"), sem("av_ps"), sem("o_done")
        sum_ps, ln_done, recip_done = sem("sum_ps"), sem("ln_done"), sem("recip_done")
        oy_done, ohi_done, olo_done = sem("oy_done"), sem("ohi_done"), sem("olo_done")
        proj_ps, res_done, x_att = sem("proj_ps"), sem("res_done"), sem("x_att")
        gate_in = [sem("gate_in0"), sem("gate_in1")]
        f1_ps, gelu_done, ghi_done, glo_done = sem("f1_ps"), sem("gelu_done"), sem("ghi_done"), sem("glo_done")
        f2_ps, f2b_done, f2g_done, x_mlp = sem("f2_ps"), sem("f2b_done"), sem("f2g_done"), sem("x_mlp")
        out_done = sem("out_done")

        def chunks(layer, phase):
            if phase == 0:
                w = A[f"wqkv{layer}"]
                return [(w[:, 0, :], wqkv[:, 0, :], wqkv[:, 3, :]), (w[:, 1, :], wqkv[:, 1, :], wqkv[:, 4, :]),
                        (w[:, 2, :], wqkv[:, 2, :], None),
                        (A[f"wproj{layer}"].rearrange("p g n -> p (g n)"),
                         wproj[:, 0, :, :].rearrange("p g n -> p (g n)"),
                         wproj[:, 1, :, :].rearrange("p g n -> p (g n)"))]
            w = A[f"w1{layer}"]
            got = [(w[:, 0, :], w1[:, 0, :], w1[:, 3, :]), (w[:, 1, :], w1[:, 1, :], w1[:, 4, :]),
                   (w[:, 2, :], w1[:, 2, :], None)]
            for c in range(3):
                got.append((A[f"w2{layer}"][:, 3 * c:3 * c + 3, :].rearrange("p g n -> p (g n)"),
                            w2[:, 0, 3 * c:3 * c + 3, :].rearrange("p g n -> p (g n)"),
                            w2[:, 1, 3 * c:3 * c + 3, :].rearrange("p g n -> p (g n)")))
            return got

        def chunk_base(layer, phase):
            return 10 * layer + 4 * phase

        def chunk_end(layer, phase):
            return chunk_base(layer, phase) + (4 if phase == 0 else 6)

        def stack_count(B, back):
            use = B.pair + 4 * B.layer + (1 if B.par or not back else 0)
            return use * (STACK_DMAS * 16)

        def gate_count(B, phase):
            return (B.pair + (4 * (2 * B.layer + phase) + 1)) * 16

        def q_of(B, phase):
            return B.qa if phase == 0 else B.qm

        block = ctx.enter_context(nc.Block())

        @block.sync
        def _(sp):
            x_view = A["x"].rearrange("(k a) (t p) d -> p k a t d", a=2, p=P)
            out_view = out.rearrange("(k a) (t p) d -> p k a t d", a=2, p=P)
            gates_view = gates_dram.rearrange("l (k a) g d -> l k a g d", a=2)

            def store_gates(layer):
                sp.wait_ge(ada_rowed, 4 * layer + 4)
                if layer == 1:
                    sp.wait_ge(tanh_done, 1)
                sp.dma_start(gates_dram[layer].rearrange("b g d -> b (g d)"),
                             ada_row[:, 4 * ADA_KIND:ADA]).then_inc(gates_out, 16)
                sp.wait_ge(gates_out, 16 * (layer + 1))

            def load_weights(layer, phase):
                for c, (src, hi, _lo) in enumerate(chunks(layer, phase)):
                    k = chunk_base(layer, phase) + c
                    wait(sp, w_lo, k - STAGES + 1)
                    sp.dma_start(stage[:, k % STAGES, 0:src.shape[1]], src).then_inc(w_in[k % STAGES], 16)

            def load_gate(B, phase):
                if phase == 0:
                    if isinstance(B.b, int) and B.b < 2:
                        wait(sp, f2g_done, NT * (NB * B.layer - 1 + B.b) if B.layer else 0)
                    else:
                        wait(sp, res_done, (B.n - 1) * NT)
                elif isinstance(B.b, int) and B.b < 2:
                    sp.wait_ge(res_done, NT * (NB * (B.layer + 1) - 1 + B.b))
                else:
                    wait(sp, f2g_done, (B.n - 1) * NT)
                sp.dma_start(gate[:, B.par, :],
                             gates_view[B.layer, B.pair, B.par, phase, :].partition_broadcast(P)
                             ).then_inc(gate_in[B.par], 16)

            def stack_rows(B, side, free):
                made = held(sp, B.n * 3 + (side + 1))
                if side == 0:
                    wait(sp, st_ps, free)
                sp.wait_ge(qkhi_done, made)
                hi = qk_hi[0:BLK, side, :, :].rearrange("p a t -> p (a t)").bitcast(F32)
                lo = qk_lo[0:BLK, side, :, :].rearrange("p a t -> p (a t)").bitcast(F32)
                for r, part in zip((0, 1, 2) if side == 0 else (0, 2, 1), (hi, hi, lo)):
                    if part is lo:
                        sp.wait_ge(qklo_done, made)
                    to = stack[DH * r:DH * r + DH, B.par, side, 0:2 * BH, :].rearrange("d (h a) t -> d h (a t)", a=2)
                    sp.dma_start(to.bitcast(F32), part).then_inc(stack_in[B.par], 16)

            def stack_tail(B, free):
                made = held(sp, B.n * 3 + 3)
                wait(sp, st_ps, free)
                sp.wait_ge(qkhi_done, made)
                hi = qk_hi[TAIL:BLK, 2, :, :].bitcast(F32)
                lo = qk_lo[TAIL:BLK, 2, :, :].bitcast(F32)
                to = lambda r, side: stack[DH * r:DH * r + DH, B.par, side, 2 * BH:H, :].bitcast(F32)
                sp.dma_start(to(0, 0), hi[:, 0, :]).then_inc(stack_in[B.par], 16)
                sp.dma_start(to(0, 1), hi[:, 1, :]).then_inc(stack_in[B.par], 16)
                sp.dma_start(to(1, 0), hi[:, 0, :]).then_inc(stack_in[B.par], 16)
                sp.dma_start(to(2, 1), hi[:, 1, :]).then_inc(stack_in[B.par], 16)
                sp.wait_ge(qklo_done, made)
                sp.dma_start(to(2, 0), lo[:, 0, :]).then_inc(stack_in[B.par], 16)
                sp.dma_start(to(1, 1), lo[:, 1, :]).then_inc(stack_in[B.par], 16)

            def max_row(B, half):
                sp.wait_ge(negmax_done, B.n * 2 + (half + 1))
                sp.dma_start(stack[KSUM:KSUM + 1, B.par, 0, 8 * half:8 * half + 8, :].bitcast(F32),
                             negmax[:, half, :].bitcast(F32)).then_inc(maxrow_in[half], 16)

            def v_to_dram(B):
                sp.wait_ge(v_done, (B.n + 1) * NT)
                sp.dma_start(v_dram[B.par].rearrange("(t p) d -> p t d", t=NT), v_rows[:, :, :]
                             ).then_inc(vrow_out, 16)

            def v_to_groups(B):
                sp.wait_ge(vrow_out, (B.n + 1) * 16)
                wait(sp, av_ps, B.n * NG - NG if isinstance(B.n, int) else B.n * NG + (-NG))
                sp.dma_start(v_group[:, B.par, :, 0:DH],
                             v_dram[B.par].rearrange("(j g) (h d) -> h j g d", j=TG, h=H)).then_inc(v_in[B.par], 16)

            def max_row_tok(B):
                sp.wait_ge(negmax_done, B.n * 2 + 2)
                for half in range(2):
                    sp.dma_start(stack[KSUM:KSUM + 1, B.par, 0, 8 * half:8 * half + 8, :].bitcast(F32),
                                 negmax_tok[64 * half:64 * half + 64, :].bitcast(F32)).then_inc(maxrow_in[half], 16)

            def attention(layer):
                def step(k, i):
                    st = Stages(layer, k, i)
                    if layer == 1 and st.has_c:
                        max_row(st.c, 1)
                    if st.has_c:
                        load_gate(st.c, 0)
                    if layer == 1 and st.has_b:
                        max_row(st.b, 0)
                    if st.has_a:
                        if i == -2:
                            sp.wait_ge(zeroed, 6 if layer == 0 else 9)
                        full = H if layer == 0 else 2 * BH
                        stack_rows(st.a, 0, st.c.n * H + full if st.has_c else 0)
                        stack_rows(st.a, 1, 0)
                    if layer == 0 and st.has_b:
                        max_row_tok(st.b)
                    if st.has_a:
                        stack_tail(st.a, st.c.n * H + H if st.has_c else 0)
                    if layer == 0 and st.has_b:
                        v_to_dram(st.b)
                        v_to_groups(st.b)
                    if layer == 0 and i == -2:
                        store_gates(1)
                    if i == 7:
                        for par in range(2):
                            sp.wait_ge(stack_in[par], STACK_DMAS * 16 * (NB // 2) * (layer + 1))
                        sp.wait_ge(vrow_out, NB * 16)
                        load_weights(layer, 1)
                        sp.dma_start(b2[:, :], A[f"b2{layer}"]).then_inc(b2_in, 16)
                return step

            def mlp(layer):
                tail = lambda: attention(layer)(0, 8)

                def ahead():
                    if layer == 0:
                        attention(1)(0, -3)
                def step(k, i):
                    if i >= 0:
                        f = Batch(layer, k, i)
                        load_gate(f, 1)
                    if layer == 0 and i == 6:
                        load_weights(1, 0)
                mlp_steps(sp, step, tail, ahead)

            sp.dma_start(c_t[:, :, :], A["c_t"]).then_inc(ada_in, 16)
            sp.dma_start(ada_w[:, :, :], A["ada_w0"]).then_inc(ada_w_in, 16)
            sp.dma_start(x_sb[:, 0, :, :, :], x_view[:, 0, :, :, :]).then_inc(x_first, 16)
            sp.dma_start(ada_b[:, :], A["ada_b0"]).then_inc(ada_b_in, 16)
            sp.dma_start(ident[:, :], A["ident"]).then_inc(const_in, 16)
            sp.dma_start(sumsel[:, :], A["sumsel"]).then_inc(const_in, 16)
            sp.dma_start(mask_x[:, :], A["mask_x"]).then_inc(const_in, 16)
            sp.dma_start(mask_w[:, :], A["mask_w"]).then_inc(const_in, 16)
            sp.dma_start(gains[:, :], A["gains"]).then_inc(const_in, 16)
            sp.dma_start(apart[:, :, :], A["apart"]).then_inc(const_in, 16)
            load_weights(0, 0)
            sp.wait_ge(zeroed, 4)
            sp.wait_ge(apart_rounded, 1)
            for par in range(2):
                for side in range(2):
                    sp.dma_start(stack[MROW:MROW + TG, par, side, :, :].bitcast(F32),
                                 apart_r[:, side, :].bitcast(F32).unsqueeze(1).to_broadcast([TG, H, TOK])
                                 ).then_inc(mask_in, 16)
            for k in range(1, NB // 2):
                sp.dma_start(x_sb[:, k, :, :, :], x_view[:, k, :, :, :]).then_inc(x_rest, 16)
            sp.wait_ge(ada_rowed, 4)
            sp.dma_start(ada_w[:, :, :], A["ada_w1"]).then_inc(ada_w_in, 16)
            sp.dma_start(ada_b[:, :], A["ada_b1"]).then_inc(ada_b_in, 16)
            store_gates(0)
            for layer in range(2):
                attention_steps(sp, attention(layer), -3 if layer == 0 else -2)
                mlp(layer)
            for k in range(NB // 2):
                sp.wait_ge(x_mlp, NT * (NB + 2 * k + 2))
                sp.dma_start(out_view[:, k, :, :, :], x_sb[:, k, :, :, :]).then_inc(out_done, 16)
            sp.wait_ge(out_done, 16 * (NB // 2))

        @block.gpsimd
        def _(pool):
            def norm_scale(B, phase):
                q = q_of(B, phase)
                pool.wait_ge(stats_done, (q + 1) * NT)
                wait(pool, z_done, q * NT * 2)
                if B.layer == 0:
                    pool.tensor_tensor(vtmp[:, :], mv[:, :, 1], floor[:, 0, :], ALU.add).then_inc(var_done, 1)
                    wait(pool, var_done, q + 1)
                else:
                    base = 2 * NB
                    pool.tensor_tensor(vtmp2[:, :], mv[:, :, 0], mv[:, :, 0], ALU.mult).then_inc(var_done, 1)
                    wait(pool, var_done, (q - base) * 3 + (base + 1))
                    pool.tensor_tensor(vtmp2[:, :], vtmp2[:, :], mv[:, :, 1], ALU.add).then_inc(var_done, 1)
                    wait(pool, var_done, (q - base) * 3 + (base + 2))
                    pool.tensor_tensor(floor[:, 1, :], neg_half[:, :], neg_half[:, :], ALU.mult)
                    pool.tensor_scalar(vtmp[:, :], vtmp2[:, :], EPS1 * EPS1 / D, None, ALU.max).then_inc(var_done, 1)
                    wait(pool, var_done, (q - base) * 3 + (base + 3))
                pool.tensor_tensor(rstd[:, :], vtmp[:, :], neg_half[:, :], ALU.pow).then_inc(rstd_done, 1)

            def h_lo(B, phase):
                q = q_of(B, phase)
                pool.wait_ge(hs_hi, q + 1)
                pool.tensor_tensor(hs[:, B.par, 3:5, :], y[:, 0:2, :], hs[:, B.par, 0:2, :].bitcast(F32),
                                   ALU.subtract).then_inc(hs_lo, 1)

            def qk_norm(B, t):
                m = B.n - NB
                pool.wait_ge(rs_chain, (m + 1) * 12)
                for side in range(2):
                    row = qk_row[:, t, side * D:side * D + 2 * BLK].rearrange("p (b d h) -> p b d h", b=2, d=DH)
                    r = rs[:, t, side * H:side * H + 2 * BH].rearrange("p (b h) -> p b h", b=2)
                    for b in range(2):
                        pool.tensor_tensor(row[:, b, :, :], row[:, b, :, :],
                                           r[:, b, :].unsqueeze(1).to_broadcast([P, DH, BH]), ALU.mult)
                    row = qk_row[:, t, side * D + 2 * BLK:(side + 1) * D].rearrange("p (d h) -> p d h", d=DH)
                    r = rs[:, t, side * H + 2 * BH:(side + 1) * H]
                    last = pool.tensor_tensor(row, row, r.unsqueeze(1).to_broadcast([P, DH, TAILH]), ALU.mult)
                last.then_inc(norm_done, 1)

            def qk_low(B, unit):
                rows = BLK
                pool.wait_ge(qkhi_done, B.n * 3 + (unit + 1))
                pool.tensor_tensor(qk_lo[0:rows, unit, :, :], qk_y[0:rows, unit, :, :],
                                   qk_hi[0:rows, unit, :, :].bitcast(F32), ALU.subtract).then_inc(qklo_done, 1)

            def o_low(B, g):
                pool.wait_ge(ohi_done, B.n * NG + (g + 1))
                pool.tensor_tensor(o_lo[:, B.par, g, :], o_y[:, g % 2, :], o_hi[:, B.par, g, :].bitcast(F32),
                                   ALU.subtract).then_inc(olo_done, 1)

            def add_attention(B, t):
                pool.wait_ge(res_done, B.n * NT + (t + 1))
                xt = x_sb[:, B.pair, B.par, t, :]
                pool.tensor_tensor(xt, xt, res[:, t, :], ALU.add).then_inc(x_att, 1)

            def attention(layer):
                def step(k, i):
                    st = Stages(layer, k, i)
                    for s in range(SLOTS):
                        for g in groups_at(layer, st, s, DIVIDE):
                            o_low(*g)
                        if st.has_n and s == NORM[layer] + 1:
                            norm_scale(st.n, 0)
                            if layer == 1 and i == -2:
                                pool.wait_ge(f2_ps, NT * NB)
                                pool.memset(big[:, 0, 1, :].bitcast(F32), 0.0).then_inc(zeroed, 1)
                                pool.wait_ge(zeroed, 8)
                                pool.memset(big[KSUM:KSUM + 1, 0, 1, :].bitcast(F32), 1.0).then_inc(zeroed, 1)
                                pool.wait_ge(zeroed, 9)
                        if st.has_n and s == SPLIT_H[layer]:
                            h_lo(st.n, 0)
                        if st.has_t and s - 2 in PROJECT[layer]:
                            add_attention(st.t, PROJECT[layer].index(s - 2))
                        if st.has_a and layer == 1 and s in (7, 8):
                            qk_norm(st.a, s - 7)
                        if st.has_a and HEADS_T[layer] + 2 <= s < HEADS_T[layer] + 5:
                            qk_low(st.a, s - HEADS_T[layer] - 2)
                return step

            def g_low(B, j):
                pool.wait_ge(ghi_done, B.n * 3 + (j + 1))
                par = (B.par + j) % 2
                pool.tensor_tensor(g_lo[:, B.par, 3 * j:3 * j + 3, :], g_y[:, par, :, :],
                                   g_hi[:, B.par, 3 * j:3 * j + 3, :].bitcast(F32), ALU.subtract).then_inc(glo_done, 1)

            def add_mlp(B, t):
                pool.wait_ge(f2g_done, B.n * NT + (t + 1))
                xt = x_sb[:, B.pair, B.par, t, :]
                pool.tensor_tensor(xt, xt, res[:, t, :], ALU.add).then_inc(x_mlp, 1)

            def mlp(layer):
                tail = lambda: attention(layer)(0, 8)

                def ahead():
                    if layer == 0:
                        attention(1)(0, -3)
                def step(k, i):
                    d, e, f = Batch(layer, k, i + 2), Batch(layer, k, i + 1), Batch(layer, k, i)
                    if i + 2 <= 7:
                        norm_scale(d, 1)
                    if i == -2:
                        tail()
                    if 0 <= i + 1 <= 7:
                        g_low(e, 0)
                    if i + 2 <= 7:
                        h_lo(d, 1)
                    if 0 <= i:
                        add_mlp(f, 0)
                    if 0 <= i + 1 <= 7:
                        g_low(e, 1)
                        g_low(e, 2)
                    if 0 <= i:
                        add_mlp(f, 1)
                    if layer == 0 and i == -1:
                        pool.wait_ge(st_ps, NB * H)
                        pool.wait_ge(glo_done, 3)
                        pool.memset(big[32:64, 1, 1, :].bitcast(F32), 0.0).then_inc(zeroed, 1)
                        pool.wait_ge(zeroed, 7)
                mlp_steps(pool, step, lambda: None, ahead)

            pool.sem_inc(x_att, FREE)
            pool.memset(floor[:, 0, :], EPS0).then_inc(const_set, 1)
            pool.memset(neg_half[:, :], -0.5).then_inc(const_set, 1)
            pool.wait_ge(const_set, 2)
            for par in range(2):
                for side in range(2):
                    pool.memset(big[:, par, side, :].bitcast(F32), 0.0).then_inc(zeroed, 1)
            pool.wait_ge(zeroed, 4)
            for par in range(2):
                pool.memset(big[KSUM:KSUM + 1, par, 1, :].bitcast(F32), 1.0).then_inc(zeroed, 1)
                pool.wait_ge(zeroed, 5 + par)
            for layer in range(2):
                attention_steps(pool, attention(layer), -3 if layer == 0 else -2)
                mlp(layer)

        @block.scalar
        def _(act):
            def split_hi(layer, phase, first=0, end=None):
                for c, (src, hi, _lo) in list(enumerate(chunks(layer, phase)))[first:end]:
                    k = chunk_base(layer, phase) + c
                    act.wait_ge(w_in[k % STAGES], 16 * (k // STAGES + 1))
                    if phase == 1:
                        act.wait_ge(st_ps, (NB * (layer + 1) - (1 if c < 3 else 0)) * H)
                    act.activation(hi, stage[:, k % STAGES, 0:src.shape[1]], ACT.Copy).then_inc(w_hi, 1)

            def modulate(B, phase):
                q = q_of(B, phase)
                wait(act, hs_rem, q)
                wait(act, hs_lo, q)
                for blk in range(3):
                    rows = P if blk < 2 else 3 * REM
                    act.wait_ge(zt_ps, q * 2 + (1 if blk < 2 else 2))
                    src = ps[0:rows, BANK_A[0], blk * TOK:(blk + 1) * TOK] if blk < 2 else ps[0:rows, BANK_A[1], 0:TOK]
                    act.activation(y[0:rows, blk, :], src, ACT.Identity,
                                   bias=mod[0:rows, B.layer, 2 * phase, blk, B.pair, B.par:B.par + 1],
                                   scale=mod[0:rows, B.layer, 2 * phase + 1, blk, B.pair, B.par:B.par + 1]
                                   ).then_inc(y_done, 1)

            def qk_out(B, t, side):
                act.wait_ge(qk_ps, B.n * 4 + (2 * t + side + 1))
                if t == 0 and side == 0:
                    wait(act, qkt_ps, B.n * 3)
                bank = BANK_A[side]
                act.activation(qk_row[:, t, side * D:(side + 1) * D], ps[:, bank, 0:D], ACT.Copy
                               ).then_inc(row_done, 1)

            def squares(B, t):
                m = B.n - NB
                act.wait_ge(row_done, B.n * 4 + (2 * t + 2))
                wait(act, ss_done, m * NT + t)
                act.activation(sq[:, :], qk_row[:, t, :], ACT.Square).then_inc(sq_done, 1)

            def heads_out(B, unit):
                act.wait_ge(qkt_ps, B.n * 3 + (unit + 1))
                wait(act, qklo_done, B.n * 3 - 2 + unit if isinstance(B.n, int) else B.n * 3 + (unit - 2))
                rows, bank = BLK, BANK_A[unit % 2]
                if unit < 2:
                    act.activation(qk_y[0:rows, unit, :, :].rearrange("p a t -> p (a t)"), ps[0:rows, bank, :],
                                   ACT.Copy, scale=qk_gain[0:rows, B.layer, unit:unit + 1]).then_inc(qky_done, 1)
                else:
                    act.activation(qk_y[0:rows, 2, 0, :], ps[0:rows, bank, 0:TOK], ACT.Copy,
                                   scale=qk_gain[0:rows, B.layer, 0:1])
                    act.activation(qk_y[0:rows, 2, 1, :], ps[0:rows, bank, TOK:2 * TOK], ACT.Copy,
                                   scale=qk_gain[0:rows, B.layer, 1:2]).then_inc(qky_done, 1)

            def v_out(B, t):
                act.wait_ge(v_ps, B.n * NT + (t + 1))
                act.wait_ge(av_ps, B.n * NG + (-NG))
                act.activation(v_sb[:, B.par, t, :, 0:DH],
                               ps[:, BANK_A[t], 0:D].rearrange("p (h d) -> p h d", h=H), ACT.Copy).then_inc(v_done, 1)

            def negate_max(B, half):
                act.wait_ge(maxt_ps, (B.n - NB) * 2 + (half + 1))
                wait(act, maxrow_in[half], B.n * 16)
                act.activation(negmax[:, half, :], ps[0:8, BANK_AV, TOK:2 * TOK], ACT.Copy, scale=-1.0
                               ).then_inc(negmax_done, 1)

            def negate_max_tok(B):
                act.wait_ge(max_done, B.n * H + H)
                for half in range(2):
                    wait(act, maxrow_in[half], B.n * 16)
                act.activation(negmax_tok[:, :], mx_tok[:, :], ACT.Copy, scale=-1.0).then_inc(negmax_done, 2)

            def exps_tok(B, e):
                act.wait_ge(st_ps, B.n * H + 2 * e + 2)
                wait(act, av_ps, B.n * NG + (e // 2 - 1))
                act.activation(prob[:, e % 4 * 2:e % 4 * 2 + 2, 0, :],
                               ps[:, BANK_ST[e % 2], :].rearrange("p (a t) -> p a t", a=2), ACT.Exp
                               ).then_inc(exp_done, 2)

            def exps(B, h):
                act.wait_ge(st_ps, B.n * H + (h + 1))
                g = h // GH
                wait(act, av_ps, B.n * NG + (g - 1))
                act.activation(prob[:, h % (2 * GH), :, :].rearrange("p a t -> p (a t)"),
                               ps[:, BANK_ST[h % 2], :], ACT.Exp).then_inc(exp_done, 1)

            def o_copy(B, g):
                act.wait_ge(av_ps, B.n * NG + (g + 1))
                wait(act, oy_done, B.n * NG + (g - 1))
                act.activation(o_sb[:, g % 2, :], ps[:, BANK_AV, 0:TOK], ACT.Copy).then_inc(o_done, 1)

            def reciprocals(B, g):
                act.wait_ge(sum_ps, B.n * NG + (g + 1))
                wait(act, recip_done, B.n * NG + g)
                act.activation(lnsum[:, :], ps[:, BANK_C, 0:TOK], ACT.Ln).then_inc(ln_done, 1)
                act.wait_ge(ln_done, B.n * NG + (g + 1))
                wait(act, oy_done, B.n * NG + (g - 1))
                act.activation(recip[:, g % 2, :], lnsum[:, :], ACT.Exp, scale=-1.0).then_inc(recip_done, 1)

            def attention(layer):
                def step(k, i):
                    st = Stages(layer, k, i)
                    if i in (-1, 1):
                        act.preload_act_table_set(LN_SET)
                    for s in range(SLOTS):
                        if st.has_c and layer == 0 and s < 8:
                            exps_tok(st.c, s)
                        if st.has_c and layer == 1:
                            exps(st.c, s)
                        for g in groups_at(layer, st, s, O_COPY):
                            o_copy(*g)
                        for g in groups_at(layer, st, s, RECIP):
                            reciprocals(*g)
                        if st.has_n and s == Z_T[layer] + 1:
                            modulate(st.n, 0)
                        if i == 7 and s == W1_SPLIT:
                            split_hi(layer, 1, 0, 3)
                        if st.has_a and s - 1 in QK[layer]:
                            t = QK[layer].index(s - 1)
                            qk_out(st.a, t, 0)
                            qk_out(st.a, t, 1)
                        if st.has_a and layer == 1 and s - 2 in QK[layer]:
                            squares(st.a, QK[layer].index(s - 2))
                        if st.has_a and HEADS_T[layer] + 1 <= s < HEADS_T[layer] + 4:
                            heads_out(st.a, s - HEADS_T[layer] - 1)
                        if st.has_b and layer == 1 and s == V[layer] + 1:
                            v_out(st.b, 0)
                            v_out(st.b, 1)
                        if st.has_b and layer == 0 and s == MAX_TOK + 8:
                            negate_max_tok(st.b)
                        if layer == 1 and st.has_c and s == 4:
                            negate_max(st.c, 1)
                        if layer == 1 and st.has_b and s == 12:
                            negate_max(st.b, 0)
                    if layer == 0 and i == -2:
                        act.wait_ge(ada_rowed, 8)
                        gates = ada_row[:, 4 * ADA_KIND:ADA]
                        act.activation(gates, gates, ACT.Tanh).then_inc(tanh_done, 1)
                        act.wait_ge(gates_out, 32)
                return step

            def gelus(B, m):
                j = m // 3
                act.wait_ge(f1_ps, B.n * NM + (m + 1))
                if m % 3 == 0:
                    wait(act, glo_done, B.n * 3 + (j - 1))
                func = ACT.Gelu if B.layer == 0 else ACT.Gelu_apprx_tanh
                act.activation(g_y[:, (B.par + j) % 2, m % 3, :], ps[:, BANK_F1[m % 3], 0:TOK], func
                               ).then_inc(gelu_done, 1)

            def mlp(layer):
                tail = lambda: attention(layer)(0, 8)

                def ahead():
                    if layer == 0:
                        attention(1)(0, -3)
                def step(k, i):
                    d, e = Batch(layer, k, i + 2), Batch(layer, k, i + 1)
                    if i == -2:
                        modulate(d, 1)
                        split_hi(layer, 1, 3)
                    if layer == 0 and i == 6:
                        split_hi(1, 0)
                    if 0 <= i + 1 <= 7:
                        for m in range(5):
                            gelus(e, m)
                    if -2 < i and i + 2 <= 7:
                        modulate(d, 1)
                    if 0 <= i + 1 <= 7:
                        for m in range(5, NM):
                            gelus(e, m)
                mlp_steps(act, step, tail, ahead)

            act.wait_ge(ada_in, 16)
            act.activation(c_e[:, :, :], c_t[:, :, :], ACT.Exp, scale=-1.0).then_inc(c_chain, 1)
            split_hi(0, 0)
            for layer in range(2):
                if layer == 1:
                    act.wait_ge(x_mlp, NT * NB)
                attention_steps(act, attention(layer), -3 if layer == 0 else -2)
                mlp(layer)

        @block.vector
        def _(dve):
            def split_lo(layer, phase, first=0, end=None):
                for c, (src, hi, lo) in list(enumerate(chunks(layer, phase)))[first:end]:
                    k = chunk_base(layer, phase) + c
                    dve.wait_ge(w_hi, k + 1)
                    raw = stage[:, k % STAGES, 0:src.shape[1]]
                    if lo is not None:
                        dve.tensor_tensor(lo, raw, hi.bitcast(F32), ALU.subtract).then_inc(w_lo, 1)
                    else:
                        dve.scalar_tensor_tensor(out=hi, in0=hi.bitcast(F32), scalar=mask_w[:, 0:1], in1=raw,
                                                 op0=ALU.mult, op1=ALU.add).then_inc(w_lo, 1)

            def condition(layer):
                w = ADA // 4
                dve.wait_ge(ada_b_in, 16 * (layer + 1))
                for c in range(4):
                    dve.wait_ge(ada_ps, 4 * layer + c + 1)
                    if layer == 1 and c == 0:
                        dve.wait_ge(gates_out, 16)
                        dve.wait_ge(ada_tr, 1)
                    dve.tensor_tensor(ada_row[:, c * w:(c + 1) * w], ps[0:NB, c, 0:w],
                                      ada_b[:, c * w:(c + 1) * w], ALU.add).then_inc(ada_rowed, 1)
                dve.wait_ge(ada_tr, layer + 1)
                for kind in range(4):
                    for blk in range(3):
                        rows = P if blk < 2 else 3 * REM
                        o = mod[0:rows, layer, kind, blk, :, :].rearrange("p k a -> p (k a)")
                        at = (kind * 3 + blk) * NB
                        src = ps[0:rows, 0, at:at + NB]
                        if kind % 2 == 0:
                            ins = dve.tensor_copy(o, src)
                        elif layer == 0:
                            ins = dve.tensor_scalar(o, src, 1.0, None, ALU.add)
                        else:
                            ins = dve.tensor_scalar(o, src, 1.0, gains[0:rows, kind // 2:kind // 2 + 1], ALU.add, ALU.mult)
                ins.then_inc(mod_set, 1)

            def stats(B, phase):
                q = q_of(B, phase)
                if phase == 1:
                    dve.wait_ge(x_att, (B.n + 1) * NT + FREE)
                elif B.layer == 1:
                    dve.wait_ge(x_mlp, (B.n - NB + 1) * NT)
                for t in range(NT):
                    dve.bn_stats(bn[:, t, :], x_sb[:, B.pair, B.par, t, :]).then_inc(bn_done, 1)
                wait(dve, rstd_done, q)
                wait(dve, bn_done, (q + 1) * NT)
                dve.memset(waits[:, :], 0.0)
                for t in range(NT):
                    dve.bn_aggr(mv[:, t, :], bn[:, t, :]).then_inc(stats_done, 1)

            def normalize(B, phase):
                q = q_of(B, phase)
                dve.wait_ge(rstd_done, q + 1)
                dve.wait_ge(stats_done, (q + 1) * NT)
                wait(dve, zt_ps, q * 2)
                for t in range(NT):
                    xt = x_sb[:, B.pair, B.par, t, :]
                    rest = z[:, t, 2 * P:].rearrange("p (a r) -> p a r", a=3)
                    wide = xt[:, 2 * P:].unsqueeze(1).to_broadcast([P, 3, REM])
                    for o, x_in in ((z[:, t, 0:2 * P], xt[:, 0:2 * P]), (rest, wide)):
                        if B.layer == 0:
                            ins = dve.tensor_scalar(o, x_in, mv[:, t, 0:1], rstd[:, t:t + 1], ALU.subtract, ALU.mult)
                        else:
                            ins = dve.tensor_scalar(o, x_in, rstd[:, t:t + 1], None, ALU.mult)
                        ins.then_inc(z_done, 1)

            def h_hi(B, phase):
                q = q_of(B, phase)
                dve.wait_ge(y_done, (q + 1) * 3)
                if phase == 1 and isinstance(B.b, int) and B.b < 2:
                    dve.wait_ge(v_ps, (B.layer + 1) * NB * NT)
                if phase == 0 and B.layer == 1 and isinstance(B.b, int) and B.b < 2:
                    dve.wait_ge(f1_ps, NM * (NB - 1 + B.b))
                if phase == 0:
                    wait(dve, v_ps, B.n * NT - NT if isinstance(B.n, int) else B.n * NT + (-NT))
                dve.tensor_copy(hs[:, B.par, 0:3, :], y[:, :, :]).then_inc(hs_hi, 1)
                dve.wait_ge(hs_hi, q + 1)
                rem = hs[:, B.par, 2, :]
                dve.scalar_tensor_tensor(out=rem, in0=rem.bitcast(F32), scalar=mask_x[:, 0:1], in1=y[:, 2, :],
                                         op0=ALU.mult, op1=ALU.add).then_inc(hs_rem, 1)

            def v_out(B, t):
                dve.wait_ge(v_ps, B.n * NT + (t + 1))
                wait(dve, vrow_out, B.n * 16)
                dve.tensor_copy(v_rows[:, t, :], ps[:, BANK_A[t], 0:D]).then_inc(v_done, 1)

            def head_sums(B, t):
                m = B.n - NB
                dve.wait_ge(sq_done, m * NT + (t + 1))
                if t == 0:
                    wait(dve, norm_done, m * NT)
                for side in range(2):
                    dve.tensor_reduce(ss[:, t, side * H:side * H + 2 * BH].rearrange("p (b h) -> p b h", b=2),
                                      sq[:, side * D:side * D + 2 * BLK].rearrange("p (b d h) -> p b h d", b=2, d=DH),
                                      AX.X, ALU.add)
                    last = dve.tensor_reduce(ss[:, t, side * H + 2 * BH:(side + 1) * H],
                                             sq[:, side * D + 2 * BLK:(side + 1) * D].rearrange("p (d h) -> p h d", d=DH),
                                             AX.X, ALU.add)
                last.then_inc(ss_done, 1)

            def rsqrt_heads(B, between):
                m = B.n - NB
                dve.wait_ge(ss_done, (m + 1) * NT)
                chain = [0]

                def link(ins):
                    chain[0] += 1
                    ins.then_inc(rs_chain, 1)
                    if chain[0] % 4 == 0 and between:
                        head_max(*between.pop(0))
                    dve.wait_ge(rs_chain, m * 12 + chain[0])

                link(dve.tensor_scalar(ss[:, :, :], ss[:, :, :], EPS1 * EPS1, None, ALU.max))
                link(dve.tensor_scalar(rt[:, :, :].bitcast(U32), ss[:, :, :].bitcast(U32), 1, None,
                                       ALU.logical_shift_right))
                link(dve.tensor_scalar(rs[:, :, :].bitcast(I32), rt[:, :, :].bitcast(I32), -1.0, float(0x5F3759DF),
                                       ALU.mult, ALU.add))
                for _ in range(3):
                    link(dve.tensor_tensor(rt[:, :, :], rs[:, :, :], ss[:, :, :], ALU.mult))
                    link(dve.scalar_tensor_tensor(out=rt[:, :, :], in0=rt[:, :, :], scalar=-0.5, in1=rs[:, :, :],
                                                  op0=ALU.mult, op1=ALU.mult))
                    link(dve.scalar_tensor_tensor(out=rs[:, :, :], in0=rt[:, :, :], scalar=1.5, in1=rs[:, :, :],
                                                  op0=ALU.add, op1=ALU.mult))

            def qk_high(B, unit):
                rows = BLK
                dve.wait_ge(qky_done, B.n * 3 + (unit + 1))
                if unit == 0:
                    first = isinstance(B.n, int) and B.n == 0
                    if not first:
                        other = 1 - B.par
                        dve.wait_ge(stack_in[other], stack_count(B, -1))
                dve.tensor_copy(qk_hi[0:rows, unit, :, :], qk_y[0:rows, unit, :, :]).then_inc(qkhi_done, 1)

            def head_max(B, h):
                dve.wait_ge(max_ps, B.n * H + (h + 1))
                if h == 0:
                    wait(dve, maxt_ps, (B.n - NB) * 2)
                dve.tensor_reduce(mx[:, :, h], ps[:, BANK_MAX[h % 2], :].rearrange("p (a t) -> p a t", a=NT),
                                  AX.X, ALU.max).then_inc(max_done, 1)

            def group_max(B, e):
                dve.wait_ge(max_ps, B.n * H + 2 * e + 2)
                if e == 0:
                    wait(dve, negmax_done, B.n * 2)
                g = token_group(e // 2, e % 2, 0)
                dve.tensor_reduce(mx_tok[:, g:g + GH], ps[:, BANK_MAX[e % 2], :].rearrange("p (a t) -> p a t", a=GH),
                                  AX.X, ALU.max).then_inc(max_done, 2)

            def divide(B, g):
                G = B.n * NG
                dve.wait_ge(recip_done, G + (g + 1))
                wait(dve, olo_done, G + (g - 1))
                dve.tensor_tensor(o_y[:, g % 2, :], o_sb[:, g % 2, :], recip[:, g % 2, :], ALU.mult).then_inc(oy_done, 1)
                dve.wait_ge(oy_done, G + (g + 1))
                if g == 0:
                    wait(dve, proj_ps, B.n * NT - NT if isinstance(B.n, int) else B.n * NT + (-NT))
                dve.tensor_copy(o_hi[:, B.par, g, :], o_y[:, g % 2, :]).then_inc(ohi_done, 1)

            def gated(B, t):
                dve.wait_ge(proj_ps, B.n * NT + (t + 1))
                if t == 0:
                    dve.wait_ge(gate_in[B.par], gate_count(B, 0))
                if B.layer == 1 and isinstance(B.b, int) and B.b == 0:
                    dve.wait_ge(x_mlp, NT * NB)
                dve.wait_ge(x_att, B.n * NT + (t + 1 - NT + FREE))
                dve.tensor_tensor(res[:, t, :], ps[:, BANK_C, 0:D], gate[:, B.par, :], ALU.mult).then_inc(res_done, 1)

            def attention(layer):
                def step(k, i):
                    st = Stages(layer, k, i)
                    for s in range(SLOTS):
                        if st.has_n and s == NORM[layer]:
                            if layer == 0 and i == -1:
                                dve.wait_ge(x_rest, 16 * (NB // 2 - 1))
                            stats(st.n, 0)
                        if st.has_n and s == NORM[layer] + 2:
                            normalize(st.n, 0)
                        if i == 7 and s == W1_SPLIT:
                            split_lo(layer, 1, 0, 3)
                        for g in groups_at(layer, st, s, DIVIDE):
                            divide(*g)
                        if st.has_n and s == SPLIT_H[layer]:
                            h_hi(st.n, 0)
                        if st.has_t and s - 1 in PROJECT[layer]:
                            gated(st.t, PROJECT[layer].index(s - 1))
                        if st.has_b and layer == 0 and s == V[layer] + 1:
                            v_out(st.b, 0)
                            v_out(st.b, 1)
                        if st.has_a and layer == 1 and s - 3 in QK[layer]:
                            head_sums(st.a, QK[layer].index(s - 3))
                        if st.has_a and layer == 1 and s == 6:
                            rsqrt_heads(st.a, [(st.b, h) for h in max_heads(6) + max_heads(7)] if st.has_b else [])
                        if st.has_a and HEADS_T[layer] + 2 <= s < HEADS_T[layer] + 5:
                            qk_high(st.a, s - HEADS_T[layer] - 2)
                        if st.has_b and layer == 0 and MAX_TOK <= s < MAX_TOK + 8:
                            group_max(st.b, s - MAX_TOK)
                        if st.has_c and layer == 1:
                            for h in late_heads(s):
                                head_max(st.c, h)
                        if st.has_b and layer == 1 and not (st.has_a and s in (6, 7)):
                            for h in max_heads(s):
                                head_max(st.b, h)
                    if layer == 0 and i == -2:
                        condition(1)
                    if layer == 0 and i == -1:
                        dve.wait_ge(gates_out, 32)
                return step

            def g_high(B, j):
                dve.wait_ge(gelu_done, B.n * NM + 3 * (j + 1))
                if j == 0:
                    wait(dve, f2_ps, B.n * NT - NT if isinstance(B.n, int) else B.n * NT + (-NT))
                par = (B.par + j) % 2
                dve.tensor_copy(g_hi[:, B.par, 3 * j:3 * j + 3, :], g_y[:, par, :, :]).then_inc(ghi_done, 1)

            def bias_gate(B, t):
                dve.wait_ge(f2_ps, B.n * NT + (t + 1))
                if t == 0:
                    dve.wait_ge(gate_in[B.par], gate_count(B, 1))
                if t == 0:
                    dve.wait_ge(b2_in, 16 * (B.layer + 1))
                    dve.wait_ge(x_att, NT * NB * (B.layer + 1) + FREE)
                wait(dve, x_mlp, B.n * NT - NT + t + 1 if isinstance(B.n, int) else B.n * NT + (t + 1 - NT))
                dve.tensor_tensor(res[:, t, :], ps[:, BANK_F2[t], 0:D], b2[:, :], ALU.add).then_inc(f2b_done, 1)
                dve.wait_ge(f2b_done, B.n * NT + (t + 1))
                dve.tensor_tensor(res[:, t, :], res[:, t, :], gate[:, B.par, :], ALU.mult).then_inc(f2g_done, 1)

            def mlp(layer):
                tail = lambda: attention(layer)(0, 8)

                def ahead():
                    if layer == 0:
                        attention(1)(0, -3)
                def step(k, i):
                    d, e, f = Batch(layer, k, i + 2), Batch(layer, k, i + 1), Batch(layer, k, i)
                    if i + 2 <= 7:
                        stats(d, 1)
                        normalize(d, 1)
                    if i == -2:
                        tail()
                        h_hi(d, 1)
                        split_lo(layer, 1, 3)
                    if layer == 0 and i == 6:
                        split_lo(1, 0)
                    if 0 <= i + 1 <= 7:
                        if i == -1:
                            dve.wait_ge(x_att, NT * NB * (layer + 1) + FREE)
                        g_high(e, 0)
                    if -2 < i and i + 2 <= 7:
                        h_hi(d, 1)
                    if 0 <= i + 1 <= 7:
                        g_high(e, 1)
                    if 0 <= i:
                        bias_gate(f, 0)
                    if 0 <= i + 1 <= 7:
                        g_high(e, 2)
                    if 0 <= i:
                        bias_gate(f, 1)
                mlp_steps(dve, step, lambda: None, ahead)

            dve.memset(y[:, 2, :], 1.0).then_inc(gain_set, 1)
            dve.memset(qk_gain[:, 0, 0:1], float(DH) ** -0.5)
            dve.memset(qk_gain[:, 0, 1:2], 1.0).then_inc(gain_set, 1)
            dve.wait_ge(const_in, 16 * 6)
            dve.tensor_copy(apart_r[:, :, :], apart[:, :, :]).then_inc(apart_rounded, 1)
            dve.tensor_copy(qk_gain[:, 1, 0:1], gains[:, 2:3])
            dve.tensor_scalar(qk_gain[:, 1, 1:2], gains[:, 3:4], float(DH) ** 0.5, None, ALU.mult).then_inc(gain_set, 1)
            dve.wait_ge(c_chain, 1)
            dve.tensor_scalar(c_e[:, :, :], c_e[:, :, :], 1.0, None, ALU.add).then_inc(c_chain, 1)
            dve.wait_ge(c_chain, 2)
            dve.reciprocal(c_e[:, :, :], c_e[:, :, :]).then_inc(c_chain, 1)
            dve.wait_ge(c_chain, 3)
            dve.tensor_tensor(s_c[:, :, :], c_e[:, :, :], c_t[:, :, :], ALU.mult).then_inc(c_chain, 1)
            split_lo(0, 0)
            condition(0)
            dve.memset(v_sb[:, :, :, :, DH + 1:32].rearrange("p a t h e -> p (a t h) e"), 0.0)
            dve.memset(v_sb[:, :, :, :, DH:DH + 1].rearrange("p a t h e -> p (a t h) e"), 1.0).then_inc(v_ones, 1)
            for layer in range(2):
                if layer == 1:
                    dve.wait_ge(x_mlp, NT * NB)
                if layer == 0:
                    dve.wait_ge(x_first, 16)
                attention_steps(dve, attention(layer), -3 if layer == 0 else -2)
                mlp(layer)

        @block.tensor
        def _(pe):
            def condition(layer):
                pe.wait_ge(ada_w_in, 16 * (layer + 1))
                if layer == 1:
                    pe.wait_ge(mod_set, 1)
                w = ADA // 4
                for c in range(4):
                    for blk in range(3):
                        rows = P if blk < 2 else REM
                        ins = pe.matmul(ps[0:NB, c, 0:w], s_c[0:rows, blk, :],
                                        ada_w[0:rows, blk, c * w:(c + 1) * w], start=(blk == 0), stop=(blk == 2))
                    ins.then_inc(ada_ps, 1)
                pe.wait_ge(ada_rowed, 4 * layer + 4)
                pe.wait_ge(const_in, 16 * 6)
                for kind in range(4):
                    for blk in range(3):
                        rows = P if blk < 2 else 3 * REM
                        lo, at = kind * ADA_KIND + blk * P, (kind * 3 + blk) * NB
                        ins = pe.transpose(ps[0:rows, 0, at:at + NB], ada_row[:, lo:lo + rows],
                                           ident[0:NB, 0:NB])
                ins.then_inc(ada_tr, 1)

            def transpose_z(B, phase):
                q = q_of(B, phase)
                pe.wait_ge(z_done, q * 4 + 4)
                wait(pe, y_done, q * 3)
                if phase == 1 and isinstance(B.b, int) and B.b == 0:
                    pe.wait_ge(v_done, (B.layer + 1) * NB * NT)
                for blk in range(2):
                    for t in range(NT):
                        ins = pe.transpose(ps[:, BANK_A[0], blk * TOK + t * P:blk * TOK + (t + 1) * P],
                                           z[:, t, blk * P:(blk + 1) * P], ident[:, :])
                ins.then_inc(zt_ps, 1)
                for t in range(NT):
                    ins = pe.transpose(ps[0:3 * REM, BANK_A[1], t * P:(t + 1) * P], z[:, t, 2 * P:], ident[:, :])
                ins.then_inc(zt_ps, 1)

            def rows_product(bank, B, t, w, cols):
                tok = slice(t * P, (t + 1) * P)
                passes = [(0, 0, P), (1, 1, P), (0, 3, P), (1, 4, P), (3, 0, P), (4, 1, P), (2, 2, KREM)]
                for n, (a, b, rows) in enumerate(passes):
                    ins = pe.matmul(ps[:, bank, 0:D], hs[0:rows, B.par, a, tok], w[0:rows, b, cols],
                                    start=(n == 0), stop=(n == len(passes) - 1))
                return ins

            def qk(B, t, part):
                n = B.n
                if t == 0 and part == 0:
                    pe.wait_ge(hs_rem, B.qa + 1)
                    pe.wait_ge(hs_lo, B.qa + 1)
                    wait(pe, qky_done, n * 3)
                if t == 1:
                    pe.wait_ge(row_done, n * 4 + (part + 1))
                rows_product(BANK_A[part], B, t, wqkv, slice(part * D, (part + 1) * D)).then_inc(qk_ps, 1)

            def v_product(B, t):
                rows_product(BANK_A[t], B, t, wqkv, slice(2 * D, 3 * D)).then_inc(v_ps, 1)

            def heads_transpose(B, unit):
                n = B.n
                if unit == 0:
                    if B.layer == 0:
                        pe.wait_ge(row_done, n * 4 + 4)
                    else:
                        pe.wait_ge(norm_done, (n - NB) * NT + NT)
                        pe.wait_ge(row_done, n * 4 + 4)
                elif unit == 2:
                    wait(pe, qky_done, n * 3 + 1)
                bank = BANK_A[unit % 2]
                for half in range(2):
                    if unit < 2:
                        lo, rows = unit * D + half * BLK, BLK
                    else:
                        lo, rows = (half + 1) * D - BLK, BLK
                    for t in range(NT):
                        ins = pe.transpose(ps[0:rows, bank, half * TOK + t * P:half * TOK + (t + 1) * P],
                                           qk_row[:, t, lo:lo + rows], ident[:, :])
                ins.then_inc(qkt_ps, 1)

            def max_scores(B, h):
                if h == 0:
                    pe.wait_ge(stack_in[B.par], stack_count(B, 0))
                wait(pe, max_done, B.n * H + (h - 1))
                q, k = stack[0:KSUM, B.par, 0, h, :], stack[0:KSUM, B.par, 1, h, :]
                for t in range(NT):
                    ins = pe.matmul(ps[:, BANK_MAX[h % 2], t * TOK:(t + 1) * TOK], q[:, t * P:(t + 1) * P], k,
                                    start=True, stop=True)
                ins.then_inc(max_ps, 1)

            def max_scores_tok(B, e):
                if e == 0:
                    pe.wait_ge(stack_in[B.par], stack_count(B, 0))
                    if B.first:
                        pe.wait_ge(mod_set, 2)
                wait(pe, max_done, B.n * H + 2 * e - 2)
                for c in range(GH):
                    g = token_group(e // 2, e % 2, c)
                    ins = pe.matmul(ps[:, BANK_MAX[e % 2], c * P:(c + 1) * P], by_group(KSUM, B.par, 0, g),
                                    by_group(KSUM, B.par, 1, g), start=True, stop=True)
                ins.then_inc(max_ps, 2)

            def scores_tok(B, e):
                if e == 0:
                    for half in range(2):
                        pe.wait_ge(maxrow_in[half], B.n * 16 + 16)
                wait(pe, exp_done, B.n * H + 2 * e - 2)
                for c in range(GH):
                    g = token_group(e // 2, e % 2, c)
                    ins = pe.matmul(ps[:, BANK_ST[e % 2], c * P:(c + 1) * P], by_group(KSUM + 1, B.par, 1, g),
                                    by_group(KSUM + 1, B.par, 0, g), start=True, stop=True)
                ins.then_inc(st_ps, 2)

            def prob_v_tok(B, u):
                pe.wait_ge(exp_done, B.n * H + GH * (u + 1))
                wait(pe, o_done, B.n * NG + u)
                if u == 0:
                    pe.wait_ge(v_in[B.par], 16 * B.pair + 16)
                for half in range(2):
                    e = 2 * u + half
                    p4 = prob[:, e % 4 * 2:e % 4 * 2 + 2, 0, :]
                    for c in range(GH):
                        ins = pe.matmul(ps[32 * c:32 * c + 32, BANK_AV, half:TOK:2],
                                        v_group[:, B.par, token_group(u, half, c), :],
                                        p4[:, c // 2, c % 2 * P:(c % 2 + 1) * P], start=True, stop=True)
                ins.then_inc(av_ps, 1)

            def transpose_max(B, half):
                pe.wait_ge(max_done, B.n * H + 8 * (half + 1))
                wait(pe, negmax_done, B.n * 2 + half)
                for t in range(NT):
                    ins = pe.transpose(ps[0:8, BANK_AV, TOK + t * P:TOK + (t + 1) * P], mx[:, t, 8 * half:8 * half + 8], ident[:, :])
                ins.then_inc(maxt_ps, 1)

            def scores(B, h):
                if h % 8 == 0:
                    pe.wait_ge(maxrow_in[h // 8], B.n * 16 + 16)
                wait(pe, exp_done, B.n * H + (h - 1))
                q, k = stack[0:KSUM + 1, B.par, 0, h, :], stack[0:KSUM + 1, B.par, 1, h, :]
                for t in range(NT):
                    ins = pe.matmul(ps[:, BANK_ST[h % 2], t * TOK:(t + 1) * TOK], k[:, t * P:(t + 1) * P], q,
                                    start=True, stop=True)
                ins.then_inc(st_ps, 1)

            def prob_v(B, g):
                pe.wait_ge(exp_done, B.n * H + GH * (g + 1))
                wait(pe, o_done, B.n * NG + g)
                if g == 0:
                    pe.wait_ge(v_done, B.n * 2 + 2)
                for t in range(NT):
                    for j in range(GH):
                        h = GH * g + j
                        ins = pe.matmul(ps[32 * j:32 * j + 32, BANK_AV, 0:TOK], v_sb[:, B.par, t, h, :],
                                        prob[:, h % (2 * GH), t, :], start=(t == 0), stop=(t == NT - 1))
                ins.then_inc(av_ps, 1)

            def spread_sums(B, g):
                pe.wait_ge(o_done, B.n * NG + (g + 1))
                pe.matmul(ps[:, BANK_C, 0:TOK], sumsel[:, :], o_sb[:, g % 2, :], start=True, stop=True).then_inc(sum_ps, 1)

            def project(B, t):
                if t == 0:
                    pe.wait_ge(ohi_done, (B.n + 1) * NG)
                    pe.wait_ge(olo_done, (B.n + 1) * NG)
                tok, n = slice(t * P, (t + 1) * P), 0
                for g in range(NG):
                    for o, w in ((o_hi, 0), (o_hi, 1), (o_lo, 0)):
                        ins = pe.matmul(ps[:, BANK_C, 0:D], o[:, B.par, g, tok], wproj[:, w, g, :],
                                        start=(n == 0), stop=(n == 3 * NG - 1))
                        n += 1
                ins.then_inc(proj_ps, 1)

            def attention(layer):
                def step(k, i):
                    st = Stages(layer, k, i)
                    a, b, c, t_ = st.a, st.b, st.c, st.t

                    def free_a(stage):
                        if stage == "z":
                            if st.has_a and layer == 0:
                                pe.wait_ge(qky_done, a.n * 3 + 3)
                            elif st.has_a:
                                pe.wait_ge(row_done, a.n * 4 + 4)
                        elif stage == "v":
                            if st.has_n:
                                pe.wait_ge(y_done, (st.n.qa + 1) * 3)
                            elif st.has_a and layer == 1:
                                pe.wait_ge(row_done, a.n * 4 + 4)
                            elif st.has_a:
                                pe.wait_ge(qky_done, a.n * 3 + 3)
                            else:
                                pe.wait_ge(qky_done, b.n * 3 + 3)
                        elif layer == 1:
                            if st.has_b:
                                pe.wait_ge(v_done, b.n * NT + NT)
                            elif st.has_n:
                                pe.wait_ge(y_done, (st.n.qa + 1) * 3)

                    def free_c(stage, part):
                        if layer == 0:
                            if stage == "project":
                                pe.wait_ge(*((ln_done, (t_.n + 1) * NG) if part == 0 else (res_done, t_.n * NT + 1)))
                            elif part == 0:
                                if st.has_t:
                                    pe.wait_ge(res_done, (t_.n + 1) * NT)
                            else:
                                pe.wait_ge(ln_done, c.n * NG + part)
                        elif stage == "project":
                            if st.has_c:
                                pe.wait_ge(ln_done, c.n * NG + part + 1)
                            else:
                                pe.wait_ge(*((ln_done, (t_.n + 1) * NG) if part == 0 else (res_done, t_.n * NT + 1)))
                        elif part == 0:
                            wait(pe, ln_done, c.n * NG)
                        elif part == 3:
                            pe.wait_ge(ln_done, t_.n * NG + 3)
                        elif st.has_t:
                            pe.wait_ge(res_done, t_.n * NT + part)
                        else:
                            pe.wait_ge(ln_done, c.n * NG + part)

                    for s in range(SLOTS):
                        if st.has_c and layer == 1:
                            scores(c, s)
                        if st.has_c and layer == 0 and s < 8:
                            scores_tok(c, s)
                        if st.has_b and layer == 0 and MAX_TOK <= s < MAX_TOK + 8:
                            max_scores_tok(b, s - MAX_TOK)
                        if st.has_c and layer == 1:
                            for h in late_heads(s):
                                max_scores(c, h)
                        if st.has_b and layer == 1:
                            for h in max_heads(s):
                                max_scores(b, h)
                        for g in groups_at(layer, st, s, 0):
                            if layer == 1 and g[1] == 0:
                                pe.wait_ge(negmax_done, c.n * 2 + 2)
                            if layer == 1 and g[1] == 2 and st.has_b:
                                pe.wait_ge(negmax_done, b.n * 2 + 1)
                            (prob_v_tok if layer == 0 else prob_v)(*g)
                        for B, g in groups_at(layer, st, s, SUMS):
                            free_c("sums", g)
                            spread_sums(B, g)
                        if st.has_a and s in QK[layer]:
                            t = QK[layer].index(s)
                            qk(a, t, 0)
                            qk(a, t, 1)
                        if st.has_n and s == Z_T[layer]:
                            free_a("z")
                            transpose_z(st.n, 0)
                        if st.has_b and s == V[layer]:
                            free_a("v")
                            v_product(b, 0)
                            v_product(b, 1)
                        if st.has_a and HEADS_T[layer] <= s < HEADS_T[layer] + 3:
                            if s == HEADS_T[layer]:
                                free_a("heads")
                            heads_transpose(a, s - HEADS_T[layer])
                        if st.has_t and s in PROJECT[layer]:
                            t = PROJECT[layer].index(s)
                            free_c("project", t)
                            project(t_, t)
                        if layer == 1 and st.has_c and s == 3:
                            wait(pe, o_done, c.n * NG)
                            transpose_max(c, 1)
                        if layer == 1 and st.has_b and s == 11:
                            if st.has_c:
                                pe.wait_ge(o_done, c.n * NG + 2)
                            transpose_max(b, 0)
                    if layer == 0 and i == -2:
                        condition(1)
                return step

            def fc1(B, m):
                if m == 0:
                    pe.wait_ge(hs_rem, B.qm + 1)
                    pe.wait_ge(hs_lo, B.qm + 1)
                wait(pe, gelu_done, B.n * NM + (m - 2))
                cols = slice(m * P, (m + 1) * P)
                passes = [(0, 0, P), (1, 1, P), (0, 3, P), (1, 4, P), (3, 0, P), (4, 1, P), (2, 2, KREM)]
                for n, (a, b, rows) in enumerate(passes):
                    ins = pe.matmul(ps[:, BANK_F1[m % 3], 0:TOK], w1[0:rows, b, cols], hs[0:rows, B.par, a, :],
                                    start=(n == 0), stop=(n == len(passes) - 1))
                ins.then_inc(f1_ps, 1)

            def fc2(B, t):
                if t == 0:
                    pe.wait_ge(ghi_done, B.n * 3 + 3)
                    pe.wait_ge(glo_done, B.n * 3 + 3)
                wait(pe, f2b_done, B.n * NT - NT + t + 1 if isinstance(B.n, int) else B.n * NT + (t + 1 - NT))
                tok, n = slice(t * P, (t + 1) * P), 0
                for m in range(NM):
                    for g, w in ((g_hi, 0), (g_hi, 1), (g_lo, 0)):
                        ins = pe.matmul(ps[:, BANK_F2[t], 0:D], g[:, B.par, m, tok], w2[:, w, m, :],
                                        start=(n == 0), stop=(n == 3 * NM - 1))
                        n += 1
                ins.then_inc(f2_ps, 1)

            def mlp(layer):
                tail = lambda: attention(layer)(0, 8)

                def ahead():
                    if layer == 0:
                        attention(1)(0, -3)
                def step(k, i):
                    d, e, f = Batch(layer, k, i + 2), Batch(layer, k, i + 1), Batch(layer, k, i)
                    if i == -1:
                        pe.wait_ge(w_lo, chunk_base(layer, 1) + 3)
                    if i == 0:
                        pe.wait_ge(w_lo, chunk_end(layer, 1))
                    if 0 <= i + 1 <= 7:
                        for m in range(5):
                            fc1(e, m)
                    if i + 2 <= 7:
                        transpose_z(d, 1)
                    if 0 <= i:
                        fc2(f, 0)
                    if 0 <= i + 1 <= 7:
                        for m in range(5, NM):
                            fc1(e, m)
                    if i == 7:
                        ahead()
                    if 0 <= i:
                        fc2(f, 1)
                mlp_steps(pe, step, tail, lambda: None)

            pe.wait_ge(c_chain, 4)
            condition(0)
            pe.wait_ge(mod_set, 1)
            pe.wait_ge(v_ones, 1)
            for layer in range(2):
                pe.wait_ge(w_lo, chunk_end(layer, 0))
                if layer == 0:
                    pe.wait_ge(mask_in, 16 * 4)
                if layer == 1:
                    pe.wait_ge(f2b_done, NT * NB)
                attention_steps(pe, attention(layer), -3 if layer == 0 else -2)
                mlp(layer)


def kernel(**inputs):
    import concourse.bacc as bacc
    from concourse.bass_utils import run_bass_kernel_spmd as run

    a = {k: np.asarray(v) for k, v in inputs.items()}
    f32 = np.float32

    def blocks(w):
        t = np.zeros((P, 3, w.shape[1]), f32)
        t[:, 0], t[:, 1] = w[0:P], w[P:2 * P]
        for r in range(3):
            t[REM * r:REM * (r + 1), 2] = w[2 * P:]
        return t

    order = [h * DH + d for blk in (range(0, 2 * BH, 2), range(1, 2 * BH, 2), range(2 * BH, H)) for d in range(DH) for h in blk]
    cols = np.array(order + [D + o for o in order] + list(range(2 * D, 3 * D)))
    kinds = (0, 1, 3, 4)
    ada_cols = [j for kind in kinds for j in list(range(kind * D, (kind + 1) * D)) + list(range(kind * D + 2 * P, (kind + 1) * D)) * 2]
    ada_cols = np.array(ada_cols + list(range(2 * D, 3 * D)) + list(range(5 * D, 6 * D)))

    ins = {"x": np.ascontiguousarray(a["x"])}
    for layer in range(2):
        g = lambda name: a[f"L{layer}_cond_{name}"]
        turn = (lambda w: w) if layer == 0 else (lambda w: w.T)
        wqkv = blocks(turn(g("qkv_w"))[:, cols])
        wqkv[3 * REM:KREM, 2] = g("qkv_b")[cols]
        w1 = blocks(turn(g("fc1_w")))
        w1[3 * REM:KREM, 2] = g("fc1_b")
        wproj = np.zeros((P, NG, D), f32)
        pw = turn(g("proj_w")).reshape(NG, GH, DH, D)
        for j in range(GH):
            wproj[32 * j:32 * j + DH] = pw[:, j].transpose(1, 0, 2)
        wproj[DH, 0] = g("proj_b")
        ins[f"wqkv{layer}"], ins[f"w1{layer}"], ins[f"wproj{layer}"] = wqkv, w1, wproj
        ins[f"w2{layer}"] = np.ascontiguousarray(turn(g("fc2_w")).reshape(NM, P, D).transpose(1, 0, 2))
        ins[f"b2{layer}"] = np.ascontiguousarray(np.broadcast_to(g("fc2_b"), (P, D)))
        ada = np.zeros((P, 3, ADA), f32)
        aw = turn(g("ada_w"))[:, ada_cols]
        ada[:, 0], ada[:, 1], ada[0:REM, 2] = aw[0:P], aw[P:2 * P], aw[2 * P:]
        ins[f"ada_w{layer}"] = ada
        ins[f"ada_b{layer}"] = np.ascontiguousarray(np.broadcast_to(g("ada_b")[ada_cols], (NB, ADA)))
    c_t = np.zeros((P, 3, NB), f32)
    ct = a["cond_1152"].T
    c_t[:, 0], c_t[:, 1], c_t[0:REM, 2] = ct[0:P], ct[P:2 * P], ct[2 * P:]
    ins["c_t"] = c_t
    own = (np.arange(TG)[:, None] == np.arange(TOK)[None, :] // NGT)
    ins["apart"] = np.ascontiguousarray(np.broadcast_to(
        np.stack([own.astype(f32), np.where(own, 0.0, -BIG).astype(f32)], axis=1), (TG, 2, TOK)))
    ins["ident"] = np.eye(P, dtype=f32)
    rows = np.arange(P)
    ins["sumsel"] = (rows[:, None] == 32 * (rows[None, :] // 32) + DH).astype(f32)
    ins["mask_x"] = -((rows >= 2 * REM) & (rows < 3 * REM)).astype(f32)[:, None]
    ins["mask_w"] = -(((rows >= REM) & (rows < 2 * REM)) | (rows == KREM - 1)).astype(f32)[:, None]
    ins["gains"] = np.ascontiguousarray(np.broadcast_to(
        np.concatenate([a[f"L1_cond_{k}"] for k in ("g1", "g2", "qg", "kg")]), (P, 4)))

    nc = bacc.Bacc("TRN2", target_bir_lowering=False, num_devices=1)
    A = {k: nc.dram_tensor(f"in_{k}", v.shape, F32, kind="ExternalInput").ap() for k, v in ins.items()}
    out = nc.dram_tensor("out", (NB, TOK, D), F32, kind="ExternalOutput").ap()
    build(nc, A, out)
    r = run(nc, [{f"in_{k}": v for k, v in ins.items()}], core_ids=[0])
    return r.results[0]["out"]
```
